# Optimizing a Trainium2 kernel written in Bass

```python
import numpy as np
import jax
import jax.numpy as jnp

def _softmax(x, axis=-1):
    return jax.nn.softmax(x, axis=axis)

def _gelu(x):
    return jax.nn.gelu(x, approximate=True)

def _silu(x):
    return jax.nn.silu(x)

def _sigmoid(x):
    return jax.nn.sigmoid(x)

def _layernorm(x, axis=-1, eps=1e-05):
    m = jnp.mean(x, axis=axis, keepdims=True)
    v = jnp.var(x, axis=axis, keepdims=True)
    return (x - m) / jnp.sqrt(v + eps)

def _scatter_add(tgt, idx, src, axis=0):
    return tgt.at[idx].add(src)

def _segment_sum(src, seg, n):
    return jax.ops.segment_sum(src, seg, n)
kernel_name = 'mk_decoder_postln_d1_seqx_r2_418d53'

def setup_inputs(seed: int=0):
    np.random.seed(seed)
    _w = jnp.asarray

    def _rec_inputs():
        import jax
        import jax.numpy as jnp
        _rk = jax.random.key(seed)
        x = -0.0005207 + 1.001 * jax.random.normal(jax.random.fold_in(_rk, 1), (4, 1024, 512), jnp.float32)
        _lenS = 1024 - jax.random.randint(jax.random.fold_in(_rk, 7), (4,), 0, max(1, 1024 // 4) + 1, jnp.int32)
        _lenS2 = 64 - jax.random.randint(jax.random.fold_in(_rk, 8), (4,), 0, max(1, 64 // 4) + 1, jnp.int32)
        _ctx_1024P = jax.random.normal(jax.random.fold_in(_rk, 11), (4, 16, 512), jnp.float32)
        _ctx_1024c = jax.random.dirichlet(jax.random.fold_in(_rk, 511), 0.3 * jnp.ones((16,), jnp.float32), (4, 64))
        _ctx_1024t = jnp.einsum('bsk,bkd->bsd', _ctx_1024c, _ctx_1024P)
        _ctx_1024t = _ctx_1024t * jax.lax.rsqrt(jnp.mean(jnp.square(_ctx_1024t)) + 1e-12) * 0.953939
        ctx_1024 = -0.000514642 + 1.00011 * (_ctx_1024t + 0.3 * jax.random.normal(jax.random.fold_in(_rk, 611), (4, 64, 512), jnp.float32))
        return (x, ctx_1024)
    x, ctx_1024 = _rec_inputs()

    def _L0_attn_setup():
        import jax, jax.numpy as jnp
        import numpy as np
        from jax import lax
        D_MODEL = 512
        D_STATE = 16
        D_CONV = 4
        EXPAND = 2
        D_INNER = EXPAND * D_MODEL
        DT_RANK = (D_MODEL + 15) // 16
        D_FF = 4 * D_MODEL
        EPS = 1e-05
        B, L = (2, 1024)

        def _rmsnorm(x, w, eps=EPS):
            return x * lax.rsqrt(jnp.mean(x * x, axis=-1, keepdims=True) + eps) * w

        def _mamba(x, in_proj_w, conv_w, conv_b, x_proj_w, dt_proj_w, dt_proj_b, A_log, Dp, out_proj_w):
            xz = x @ in_proj_w.T
            u, z = jnp.split(xz, 2, axis=-1)
            u_nch = u.transpose(0, 2, 1)
            u_conv = lax.conv_general_dilated(u_nch, conv_w, window_strides=(1,), padding=[(D_CONV - 1, 0)], dimension_numbers=('NCH', 'OIH', 'NCH'), feature_group_count=D_INNER)
            u_conv = u_conv + conv_b[None, :, None]
            u_act = jax.nn.silu(u_conv.transpose(0, 2, 1))
            proj = u_act @ x_proj_w.T
            dt_r, Bm, Cm = jnp.split(proj, [DT_RANK, DT_RANK + D_STATE], axis=-1)
            dt = jax.nn.softplus(dt_r @ dt_proj_w.T + dt_proj_b)
            A = -jnp.exp(A_log)
            dA = jnp.exp(jnp.einsum('bld,dn->bldn', dt, A))
            dBu = jnp.einsum('bld,bln,bld->bldn', dt, Bm, u_act)

            def step(h, inputs):
                dA_t, dBu_t = inputs
                h = dA_t * h + dBu_t
                return (h, h)
            h0 = jnp.zeros((x.shape[0], D_INNER, D_STATE), x.dtype)
            _, hs = lax.scan(step, h0, (dA.transpose(1, 0, 2, 3), dBu.transpose(1, 0, 2, 3)))
            y = jnp.einsum('lbdn,bln->bld', hs, Cm) + u_act * Dp
            y = y * jax.nn.silu(z)
            return y @ out_proj_w.T
        key = jax.random.key(seed)
        ks = jax.random.split(key, 16)
        s = 0.02
        inp = {'x': jax.random.normal(ks[0], (B, L, D_MODEL), jnp.float32), 'norm1_w': jnp.ones((D_MODEL,), jnp.float32), 'norm2_w': jnp.ones((D_MODEL,), jnp.float32), 'in_proj_w': s * jax.random.normal(ks[1], (2 * D_INNER, D_MODEL), jnp.float32), 'conv_w': s * jax.random.normal(ks[2], (D_INNER, 1, D_CONV), jnp.float32), 'conv_b': jnp.zeros((D_INNER,), jnp.float32), 'x_proj_w': s * jax.random.normal(ks[3], (DT_RANK + 2 * D_STATE, D_INNER), jnp.float32), 'dt_proj_w': s * jax.random.normal(ks[4], (D_INNER, DT_RANK), jnp.float32), 'dt_proj_b': jax.random.uniform(ks[5], (D_INNER,), jnp.float32, -4.0, -2.0), 'A_log': jnp.log(jnp.broadcast_to(jnp.arange(1, D_STATE + 1, dtype=jnp.float32), (D_INNER, D_STATE))), 'D': jnp.ones((D_INNER,), jnp.float32), 'out_proj_w': s * jax.random.normal(ks[6], (D_MODEL, D_INNER), jnp.float32), 'w1': s * jax.random.normal(ks[7], (D_FF, D_MODEL), jnp.float32), 'w2': s * jax.random.normal(ks[8], (D_FF, D_MODEL), jnp.float32), 'w3': s * jax.random.normal(ks[9], (D_MODEL, D_FF), jnp.float32)}
        return inp
    _L0_attn_all = _L0_attn_setup()
    _L0_attn_in = {k: v for k, v in _L0_attn_all.items() if k in ('norm1_w', 'norm2_w', 'in_proj_w', 'conv_w', 'conv_b', 'x_proj_w', 'dt_proj_w', 'dt_proj_b', 'A_log', 'D', 'out_proj_w', 'w1', 'w2', 'w3')}
    del _L0_attn_all

    def _L0_xattn_setup():
        import jax, jax.numpy as jnp
        import numpy as np
        import math
        B, S, D, H = (1, 1024, 512, 16)
        DK = D // H
        DH = 64
        LOG_T_MIN = math.log(0.1)
        LOG_T_MAX = math.log(10.0)

        def _linear(x, W, b):
            return x @ W.T + b
        key = jax.random.key(seed)
        ks = jax.random.split(key, 20)
        p = 0.02
        return {'query': jax.random.normal(ks[0], (B, S, D), jnp.float32), 'key': jax.random.normal(ks[1], (B, S, D), jnp.float32), 'value': jax.random.normal(ks[2], (B, S, D), jnp.float32), 'Wq': jax.random.normal(ks[3], (D, D), jnp.float32) * p, 'bq': jax.random.normal(ks[4], (D,), jnp.float32) * p, 'Wk': jax.random.normal(ks[5], (D, D), jnp.float32) * p, 'bk': jax.random.normal(ks[6], (D,), jnp.float32) * p, 'Wv': jax.random.normal(ks[7], (D, D), jnp.float32) * p, 'bv': jax.random.normal(ks[8], (D,), jnp.float32) * p, 'Wo': jax.random.normal(ks[9], (D, D), jnp.float32) * p, 'bo': jax.random.normal(ks[10], (D,), jnp.float32) * p, 'w1': jax.random.normal(ks[11], (DH, 3), jnp.float32) * 0.3, 'b1': jax.random.normal(ks[12], (DH,), jnp.float32) * 0.1, 'w2': jax.random.normal(ks[13], (DH, DH), jnp.float32) * 0.1, 'b2': jax.random.normal(ks[14], (DH,), jnp.float32) * 0.1, 'w3': jax.random.normal(ks[15], (1, DH), jnp.float32) * 0.1, 'b3': jnp.full((1,), (LOG_T_MIN + LOG_T_MAX) / 2, jnp.float32)}
    _L0_xattn_all = _L0_xattn_setup()
    _L0_xattn_in = {k: v for k, v in _L0_xattn_all.items() if k in ('Wq', 'bq', 'Wk', 'bk', 'Wv', 'bv', 'Wo', 'bo', 'w1', 'b1', 'w2', 'b2', 'w3', 'b3')}
    del _L0_xattn_all

    def _L0_ffn_setup():
        import jax, jax.numpy as jnp
        import numpy as np
        TOP_K = 2
        EPS = 1e-06
        key = jax.random.key(seed)
        ks = jax.random.split(key, 6)
        B_, T, D = (8, 1024, 512)
        E, R_ = (8, 16)
        scale = 1.0 / np.sqrt(D)
        x = jax.random.normal(ks[0], (B_, T, D), dtype=jnp.float32)
        W = jax.random.normal(ks[1], (D, D), dtype=jnp.float32) * scale
        b = jax.random.normal(ks[2], (D,), dtype=jnp.float32)
        R = jax.random.normal(ks[3], (E, D), dtype=jnp.float32) * scale
        A = jax.random.normal(ks[4], (E, R_, D), dtype=jnp.float32) * scale
        B = jax.random.normal(ks[5], (D, R_), dtype=jnp.float32)[None] * jnp.ones((E, 1, 1), jnp.float32)
        B = jax.random.normal(ks[5], (E, D, R_), dtype=jnp.float32) * (1.0 / np.sqrt(R_))
        return {'x': x, 'W': W, 'b': b, 'R': R, 'A': A, 'B': B}
    _L0_ffn_all = _L0_ffn_setup()
    _L0_ffn_in = {k: v for k, v in _L0_ffn_all.items() if k in ('W', 'b', 'R', 'A', 'B')}
    del _L0_ffn_all
    return {'x': x, 'ctx_1024': ctx_1024, 'L0_attn_norm1_w': _L0_attn_in['norm1_w'], 'L0_attn_norm2_w': _L0_attn_in['norm2_w'], 'L0_attn_in_proj_w': _L0_attn_in['in_proj_w'], 'L0_attn_conv_w': _L0_attn_in['conv_w'], 'L0_attn_conv_b': _L0_attn_in['conv_b'], 'L0_attn_x_proj_w': _L0_attn_in['x_proj_w'], 'L0_attn_dt_proj_w': _L0_attn_in['dt_proj_w'], 'L0_attn_dt_proj_b': _L0_attn_in['dt_proj_b'], 'L0_attn_A_log': _L0_attn_in['A_log'], 'L0_attn_D': _L0_attn_in['D'], 'L0_attn_out_proj_w': _L0_attn_in['out_proj_w'], 'L0_attn_w1': _L0_attn_in['w1'], 'L0_attn_w2': _L0_attn_in['w2'], 'L0_attn_w3': _L0_attn_in['w3'], 'L0_xattn_Wq': _L0_xattn_in['Wq'], 'L0_xattn_bq': _L0_xattn_in['bq'], 'L0_xattn_Wk': _L0_xattn_in['Wk'], 'L0_xattn_bk': _L0_xattn_in['bk'], 'L0_xattn_Wv': _L0_xattn_in['Wv'], 'L0_xattn_bv': _L0_xattn_in['bv'], 'L0_xattn_Wo': _L0_xattn_in['Wo'], 'L0_xattn_bo': _L0_xattn_in['bo'], 'L0_xattn_w1': _L0_xattn_in['w1'], 'L0_xattn_b1': _L0_xattn_in['b1'], 'L0_xattn_w2': _L0_xattn_in['w2'], 'L0_xattn_b2': _L0_xattn_in['b2'], 'L0_xattn_w3': _L0_xattn_in['w3'], 'L0_xattn_b3': _L0_xattn_in['b3'], 'L0_ffn_W': _L0_ffn_in['W'], 'L0_ffn_b': _L0_ffn_in['b'], 'L0_ffn_R': _L0_ffn_in['R'], 'L0_ffn_A': _L0_ffn_in['A'], 'L0_ffn_B': _L0_ffn_in['B']}

def reference(x, ctx_1024, L0_attn_norm1_w, L0_attn_norm2_w, L0_attn_in_proj_w, L0_attn_conv_w, L0_attn_conv_b, L0_attn_x_proj_w, L0_attn_dt_proj_w, L0_attn_dt_proj_b, L0_attn_A_log, L0_attn_D, L0_attn_out_proj_w, L0_attn_w1, L0_attn_w2, L0_attn_w3, L0_xattn_Wq, L0_xattn_bq, L0_xattn_Wk, L0_xattn_bk, L0_xattn_Wv, L0_xattn_bv, L0_xattn_Wo, L0_xattn_bo, L0_xattn_w1, L0_xattn_b1, L0_xattn_w2, L0_xattn_b2, L0_xattn_w3, L0_xattn_b3, L0_ffn_W, L0_ffn_b, L0_ffn_R, L0_ffn_A, L0_ffn_B):
    import jax
    import jax.numpy as jnp

    def _L0_attn_ref(x, norm1_w, norm2_w, in_proj_w, conv_w, conv_b, x_proj_w, dt_proj_w, dt_proj_b, A_log, D, out_proj_w, w1, w2, w3):
        import jax, jax.numpy as jnp
        import numpy as np
        from jax import lax
        D_MODEL = 512
        D_STATE = 16
        D_CONV = 4
        EXPAND = 2
        D_INNER = EXPAND * D_MODEL
        DT_RANK = (D_MODEL + 15) // 16
        D_FF = 4 * D_MODEL
        EPS = 1e-05
        B, L = (2, 1024)

        def _rmsnorm(x, w, eps=EPS):
            return x * lax.rsqrt(jnp.mean(x * x, axis=-1, keepdims=True) + eps) * w

        def _mamba(x, in_proj_w, conv_w, conv_b, x_proj_w, dt_proj_w, dt_proj_b, A_log, Dp, out_proj_w):
            xz = x @ in_proj_w.T
            u, z = jnp.split(xz, 2, axis=-1)
            u_nch = u.transpose(0, 2, 1)
            u_conv = lax.conv_general_dilated(u_nch, conv_w, window_strides=(1,), padding=[(D_CONV - 1, 0)], dimension_numbers=('NCH', 'OIH', 'NCH'), feature_group_count=D_INNER)
            u_conv = u_conv + conv_b[None, :, None]
            u_act = jax.nn.silu(u_conv.transpose(0, 2, 1))
            proj = u_act @ x_proj_w.T
            dt_r, Bm, Cm = jnp.split(proj, [DT_RANK, DT_RANK + D_STATE], axis=-1)
            dt = jax.nn.softplus(dt_r @ dt_proj_w.T + dt_proj_b)
            A = -jnp.exp(A_log)
            dA = jnp.exp(jnp.einsum('bld,dn->bldn', dt, A))
            dBu = jnp.einsum('bld,bln,bld->bldn', dt, Bm, u_act)

            def step(h, inputs):
                dA_t, dBu_t = inputs
                h = dA_t * h + dBu_t
                return (h, h)
            h0 = jnp.zeros((x.shape[0], D_INNER, D_STATE), x.dtype)
            _, hs = lax.scan(step, h0, (dA.transpose(1, 0, 2, 3), dBu.transpose(1, 0, 2, 3)))
            y = jnp.einsum('lbdn,bln->bld', hs, Cm) + u_act * Dp
            y = y * jax.nn.silu(z)
            return y @ out_proj_w.T
        h = x + _mamba(_rmsnorm(x, norm1_w), in_proj_w, conv_w, conv_b, x_proj_w, dt_proj_w, dt_proj_b, A_log, D, out_proj_w)
        xn = _rmsnorm(h, norm2_w)
        mlp = jax.nn.silu(xn @ w1.T) * (xn @ w2.T) @ w3.T
        return h + mlp

    def _L0_xattn_ref(query, key, value, Wq, bq, Wk, bk, Wv, bv, Wo, bo, w1, b1, w2, b2, w3, b3):
        import jax, jax.numpy as jnp
        import numpy as np
        import math
        B, S, D, H = (1, 1024, 512, 16)
        DK = D // H
        DH = 64
        LOG_T_MIN = math.log(0.1)
        LOG_T_MAX = math.log(10.0)

        def _linear(x, W, b):
            return x @ W.T + b
        b, sq, d = query.shape
        sk = key.shape[1]
        h, dk = (H, DK)
        Q = _linear(query, Wq, bq).reshape(b, sq, h, dk).transpose(0, 2, 1, 3)
        K = _linear(key, Wk, bk).reshape(b, sk, h, dk).transpose(0, 2, 1, 3)
        V = _linear(value, Wv, bv).reshape(b, sk, h, dk).transpose(0, 2, 1, 3)
        qk = jnp.einsum('bhqd,bhkd->bhqk', Q, K)
        scores = qk / math.sqrt(dk)
        mean_sim = scores.mean(axis=(-2, -1))
        max_sim = scores.max(axis=-1).mean(axis=-1)
        probs = jax.nn.softmax(scores, axis=-1)
        entropy_proxy = jnp.var(probs, axis=-1, ddof=1).mean(axis=-1)
        feats = jnp.stack([mean_sim, max_sim, entropy_proxy], axis=-1)
        hidden = jax.nn.gelu(_linear(feats, w1, b1), approximate=False)
        hidden = jax.nn.gelu(_linear(hidden, w2, b2), approximate=False)
        log_t = jnp.clip(_linear(hidden, w3, b3), LOG_T_MIN, LOG_T_MAX)
        t = jnp.exp(log_t)[..., None]
        attn_scores = qk / (2.0 * t)
        attn = jax.nn.softmax(attn_scores, axis=-1)
        attn = jnp.nan_to_num(attn, nan=0.0)
        out = jnp.einsum('bhqk,bhkd->bhqd', attn, V)
        out = out.transpose(0, 2, 1, 3).reshape(b, sq, d)
        return _linear(out, Wo, bo)

    def _L0_ffn_ref(x, W, b, R, A, B):
        import jax, jax.numpy as jnp
        import numpy as np
        TOP_K = 2
        EPS = 1e-06
        base_out = jnp.einsum('btd,od->bto', x, W) + b
        logits = jnp.einsum('btd,ed->bte', x, R)
        gate = jax.nn.softmax(logits, axis=-1)
        E = gate.shape[-1]
        _, idx = jax.lax.top_k(gate, TOP_K)
        mask = jax.nn.one_hot(idx, E, dtype=gate.dtype).sum(axis=-2)
        gate = gate * mask
        gate = gate / (gate.sum(axis=-1, keepdims=True) + EPS)
        h = jnp.einsum('btd,erd->bter', x, A)
        gh = gate[..., None] * h
        lora_out = jnp.einsum('bter,eor->bto', gh, B)
        return base_out + lora_out
    x = _layernorm(x + _L0_attn_ref(x, L0_attn_norm1_w, L0_attn_norm2_w, L0_attn_in_proj_w, L0_attn_conv_w, L0_attn_conv_b, L0_attn_x_proj_w, L0_attn_dt_proj_w, L0_attn_dt_proj_b, L0_attn_A_log, L0_attn_D, L0_attn_out_proj_w, L0_attn_w1, L0_attn_w2, L0_attn_w3), axis=-1)
    x = _layernorm(x + _L0_xattn_ref(x, ctx_1024, ctx_1024, L0_xattn_Wq, L0_xattn_bq, L0_xattn_Wk, L0_xattn_bk, L0_xattn_Wv, L0_xattn_bv, L0_xattn_Wo, L0_xattn_bo, L0_xattn_w1, L0_xattn_b1, L0_xattn_w2, L0_xattn_b2, L0_xattn_w3, L0_xattn_b3), axis=-1)
    x = _layernorm(x + _L0_ffn_ref(x, L0_ffn_W, L0_ffn_b, L0_ffn_R, L0_ffn_A, L0_ffn_B), axis=-1)
    return x

_drawn_inputs = setup_inputs


def setup_inputs(seed=0):
    import zlib

    import numpy as np

    out = dict(_drawn_inputs(seed))
    spreads = {'L0_attn_norm1_w': (1.0, 0.6),
     'L0_attn_norm2_w': (1.0, 0.2),
     'L0_attn_conv_b': (0.0, 0.404),
     'L0_attn_D': (1.0, 0.6)}
    factors = {'L0_attn_in_proj_w': 3.246,
     'L0_attn_conv_w': 8.0,
     'L0_attn_x_proj_w': 8.0,
     'L0_attn_dt_proj_w': 8.0,
     'L0_attn_dt_proj_b': 8.0,
     'L0_attn_A_log': 8.0,
     'L0_attn_out_proj_w': 3.037,
     'L0_xattn_bq': 5.658,
     'L0_xattn_bk': 8.0,
     'L0_xattn_w1': 8.0,
     'L0_xattn_b1': 8.0,
     'L0_xattn_w2': 8.0,
     'L0_xattn_b2': 8.0,
     'L0_xattn_w3': 4.948}
    for name, (base, spread) in spreads.items():
        noise = np.random.default_rng([zlib.crc32(name.encode()), seed]).standard_normal(out[name].shape)
        drawn = base * np.exp(spread * noise) if base else spread * noise
        out[name] = jnp.asarray(drawn.astype(out[name].dtype))
    for name, factor in factors.items():
        out[name] = (out[name] * factor).astype(out[name].dtype)
    return out
```

```python
import numpy as np
import concourse.bass as bass
from concourse import mybir
from contextlib import ExitStack

P = 128
BATCH, SEQ, DM, DI, NS, DTR, DFF = 4, 1024, 512, 1024, 16, 32, 2048
HEADS, KEYS, HID = 16, 64, 64
DK = DM // HEADS
EXPERTS, RANK = 8, 16
CH = 512
CHUNKS = BATCH * SEQ // CH
TT = CH // P
KC = DM // P
JB = DI // P
FB = DFF // P
NP = 2
NG = NS // NP
STEPS = NG * JB
FILLS = 38
WSLOTS = 3
EPS = 1e-5
LOG_T = float(np.log(10.0))
CONSTS = 17
GUARD = 2.0 ** -26

MLP = [("mlp", f) for f in range(FB)] + [("mlp_last", 0)]
DENSE0 = MLP + [("norm", 0), ("turn", 0), ("query", 0)] + [("stats", t) for t in range(4)]
DENSE1 = (MLP + [("norm", 1), ("turn", 1), ("query", 1)] + [("stats", t) for t in range(4, 8)]
          + [("temperature", 0), ("score", 0)]
          + [u for t in range(8) for u in ([("score", t + 1)] if t < 7 else []) + [("attend", t)]]
          + [("norm", 2), ("norm", 3), ("turn", 2), ("mix", 0), ("norm", 4), ("turn", 3), ("mix", 1), ("norm", 5)])
LOADS_DENSE0 = [("ff", f) for f in range(FB)] + [("wq", 0)]
LOADS_DENSE1 = [("ff", f) for f in range(FB)] + [("wq", 0), ("wo", 0), ("wf", 0)]
LOADS_FRONT = [("in", 0), ("in", 1)]
LOADS_CLOSE = [("in", 2), ("in", 3), ("out", 0), ("out", 1)]
FIRST = LOADS_FRONT + LOADS_CLOSE + LOADS_FRONT + LOADS_DENSE0 + LOADS_CLOSE
BODY = LOADS_FRONT + LOADS_DENSE1 + LOADS_CLOSE + LOADS_FRONT + LOADS_DENSE0 + LOADS_CLOSE
assert len(BODY) % WSLOTS == 0
DVE_FRONT, DVE_DENSE0, DVE_DENSE1 = 36, 19, 109


def need(eng, sem, value):
    if isinstance(value, int) and value <= 0:
        return
    eng.wait_ge(sem, value)


class Chain:

    def __init__(self, eng, sem, start):
        self.eng, self.sem, self.start, self.n = eng, sem, start, 0

    def mark(self, ins):
        self.n += 1
        ins.then_inc(self.sem, 1)

    def settle(self):
        need(self.eng, self.sem, self.start + self.n)

    def link(self, ins):
        self.mark(ins)
        self.settle()


def decoder_layer(nc, A, out):
    f32 = mybir.dt.float32
    ALU = mybir.AluOpType
    ACT = mybir.ActivationFunctionType
    AX = mybir.AxisListType.X
    ctx = ExitStack()
    with ctx:
        def sb(name, shape):
            return ctx.enter_context(nc.sbuf_tensor(name, shape, f32))

        def sem(name):
            return ctx.enter_context(nc.semaphore(name))

        ident = sb("ident", [P, P])
        w_x = sb("w_x", [P, JB, 64])
        w_dt = sb("w_dt", [DTR, DI])
        w_ra = sb("w_ra", [P, KC, EXPERTS + P])
        w_b = sb("w_b", [P, DM])
        bo_row = sb("bo_row", [P, DM])
        ffn_row = sb("ffn_row", [P, DM])
        cols = sb("cols", [P, 2 * KC + 3 * JB + KC + 4 * JB + 8])
        o = 0
        def col(n):
            nonlocal o
            o += n
            return cols[:, o - n:o]
        norm1, norm2, bq_c, bk_c0 = col(KC), col(KC), col(KC), None
        conv_b, dt_b, d_skip = col(JB), col(JB), col(JB)
        conv_w = col(4 * JB).rearrange("p (j k) -> p j k", k=4)
        rank_w = col(8)
        a_neg = sb("a_neg", [P, JB, NS])
        bk_c = sb("bk_c", [P, KC])
        t_w1 = sb("t_w1", [3, HID])
        t_w2 = sb("t_w2", [HID, P])
        t_w3 = sb("t_w3", [HID, P])
        t_w3c = sb("t_w3c", [HID, 1])
        t_b = sb("t_b", [P, 3])
        f_sc = sb("f_sc", [3, 2])
        eps_t = sb("eps_t", [P, 1])
        ones_t = sb("ones_t", [P, 1])
        zero3 = sb("zero3", [P, 3])
        wring = sb("wring", [P, WSLOTS, 2048])
        xm = sb("xm", [P, TT, DM])
        xnT = sb("xnT", [P, KC, CH])
        dt = sb("dt", [P, JB, CH])
        dtu = sb("dtu", [P, JB, CH])
        y = sb("y", [P, JB, CH])
        proj = sb("proj", [64, CH])
        bc = sb("bc", [P, 2, 2, NP, CH])
        state = sb("state", [P, JB, NS])
        halo = sb("halo", [P, JB, 3])
        scr = sb("scr", [P, 5120])
        small = sb("small", [P, 2, TT])
        res = sb("res", [P, 2, TT, DM])
        fT = sb("fT", [P, KC, CH])
        qT = sb("qT", [P, KC, SEQ])
        kbd = sb("kbd", [P, KC, 4 * KEYS])
        vbd = sb("vbd", [P, HEADS // 2, 2 * DK])
        work = sb("work", [P, 3584])
        stv = sb("stv", [P, 8, 3, HEADS])
        sta = sb("sta", [P, 3, HEADS])
        sden = sb("sden", [P, 2, HEADS])
        tmp16 = sb("tmp16", [P, 4, HEADS])
        bnst = sb("bnst", [P, TT, 6])
        mv = sb("mv", [P, TT, 2])
        sdev = sb("sdev", [P, 2, TT])
        gate = sb("gate", [P, 6, TT, EXPERTS])
        gmax = sb("gmax", [P, TT])

        da = scr[:, 0:2048].rearrange("p (r n l) -> p r n l", r=2, n=NP)
        hb = scr[:, 2048:5120].rearrange("p (r n l) -> p r n l", r=3, n=NP)
        sq_junk = scr[:, 0:2048].rearrange("p (t d) -> p t d", t=TT)
        up = scr[:, 0:1032].rearrange("p (r l) -> p r l", r=2)
        acc = scr[:, 1040:2064].rearrange("p (r l) -> p r l", r=2)
        th = scr[:, 2064:3088].rearrange("p (r l) -> p r l", r=2)
        w1p = scr[:, 0:2048].rearrange("p (j l) -> p j l", j=4)
        lnp = scr[:, 2048:4096].rearrange("p (j l) -> p j l", j=4)
        zt = scr[:, 0:1024].rearrange("p (r l) -> p r l", r=2)
        zc = scr[:, 1024:2048].rearrange("p (r l) -> p r l", r=2)
        ht = scr[:, 2048:4096].rearrange("p (t d) -> p t d", t=TT)
        t1 = work[:, 0:1024].rearrange("p (r l) -> p r l", r=2)
        hm = work[:, 1024:2048].rearrange("p (r l) -> p r l", r=2)
        sc = work[:, 0:2048].rearrange("p (r h k) -> p r h k", r=2, h=HEADS)
        scf = work[:, 0:2048].rearrange("p (r c) -> p r c", r=2)
        at = work[:, 2048:3072]
        oT = work[:, 3072:3584].rearrange("p (c t) -> p c t", c=KC)
        gh = work[:, 0:512].rearrange("p (t e r) -> p t e r", t=TT, e=EXPERTS)
        ghf = work[:, 0:512].rearrange("p (t c) -> p t c", t=TT)

        pm = ctx.enter_context(nc.psum_tensor("pm", [P, 2, 512], f32))
        pd = ctx.enter_context(nc.psum_tensor("pd", [P, 4, 512], f32))
        ph = ctx.enter_context(nc.psum_tensor("ph", [P, 2, 512], f32))
        pscore = pd[:, :, :].rearrange("p (r a) c -> p r (a c)", r=2)
        phf = ph[:, :, :].rearrange("p a c -> p (a c)")

        bc_dram = nc.dram_tensor("bc_dram", (2, 2 * NS, CH), f32, kind="Internal").ap()
        k_dram = nc.dram_tensor("k_dram", (BATCH, KC, P, KEYS), f32, kind="Internal").ap()
        v_dram = nc.dram_tensor("v_dram", (BATCH, KEYS, DM), f32, kind="Internal").ap()

        names = """const_in ctx_in zeroed kv_full kv_out kv_stored kv_loaded x_in ss_ready sd_ready
        xn_ready pm_full pm_free conv_done th_ready u_ready e_min e_exp w1_ready ln_ready dtu_ready y_init
        proj_stored da_ready dbu_ready scan_done h_ready p_ready y_half y_added gate_done ht_ready ss2_ready
        sd2_ready hn_ready h1_full h1_free t1_ready h2_full hm_ready w3_done ln_var ln_sd ln_done tr_full
        tr_out q_full q_out sc_full sc_free e_ready st_done sta_ready tm_pe tm_act tm_dve kb_scaled at_norm
        pt_full at_ready pv_full ot_ready wo_full wo_free mix_full gl_ready ge_ready gh_ready gt_full
        gt_ready mix_done res_done a_ready dve_front dve_dense act_front""".split()
        S = {n: sem(n) for n in names}
        w_in = [sem(f"w_in{i}") for i in range(WSLOTS)]
        bc_in = [sem(f"bc_in{i}") for i in range(2)]
        out_stored = [sem(f"out_stored{i}") for i in range(2)]
        s = type("Sems", (), S)

        def norm_no(b, i):
            return b * 6 + i

        def body(eng_parts, b, dense_b):
            front, scan, close, dense = eng_parts
            for half in range(2):
                front(b, half)
                units, ub = (DENSE0, b) if half else (DENSE1, dense_b)
                if ub is None:
                    units = []
                at_step = [(i * STEPS) // max(1, len(units)) for i in range(len(units))]
                n = 0
                for k in range(STEPS):
                    scan(b, half, k)
                    while n < len(units) and at_step[n] <= k:
                        dense(ub, 1 - half, *units[n])
                        n += 1
                scan(b, half, STEPS)
                close(b, half)

        def run(eng, parts, start_part=lambda it: None):
            start_part(None)
            body(parts, 0, None)
            with eng.Fori(1, BATCH) as b:
                start_part(b)
                body(parts, b, b - 1)
            start_part(BATCH)
            for u in DENSE1:
                parts[3](BATCH - 1, 1, *u)

        class Slots:

            def __init__(self):
                self.pos = 0

            def start_part(self, it):
                self.first = 0 if it is None else len(FIRST)
                self.turn0 = 0 if it is None else (it - 1) * (len(BODY) // WSLOTS)
                self.pos = 0

            def next(self):
                n = self.first + self.pos
                self.pos += 1
                return n % WSLOTS, self.turn0 + n // WSLOTS + 1

        block = ctx.enter_context(nc.Block())

        @block.sync
        def _(sp):
            for dst, src in ((ident[:, :], A["identity"]), (w_x[:, :, :], A["w_x"]), (w_dt[:, :], A["w_dt"]),
                             (w_ra[:, :, :], A["w_ra"]), (w_b[:, :], A["w_b"]),
                             (bo_row[:, :], A["bo"].partition_broadcast(P)),
                             (ffn_row[:, :], A["ffn_b"].partition_broadcast(P)),
                             (cols[:, :], A["cols"]), (a_neg[:, :, :], A["a_log"]), (bk_c[:, :], A["bk_c"]),
                             (t_w1[:, :], A["t_w1"]), (t_w2[:, 0:HID], A["t_w2"]), (t_w3c[:, :], A["t_w3"]),
                             (t_b[0:HID, 0:1], A["t_b1"]), (t_b[0:HID, 1:2], A["t_b2"]),
                             (t_b[:, 2:3], A["t_b3"].partition_broadcast(P)), (f_sc[:, :], A["f_sc"])):
                sp.dma_start(dst, src).then_inc(s.const_in, 16)
            sp.dma_start(dtu[:, 0:2, :].rearrange("p a l -> p (a l)"), A["ctxT"]).then_inc(s.ctx_in, 16)
            sp.dma_start(dt[:, 0:4, :], A["wk"]).then_inc(s.ctx_in, 16)
            sp.dma_start(dt[:, 4:8, :], A["wv"]).then_inc(s.ctx_in, 16)
            sp.dma_start(y[:, 0, :], A["bv"].partition_broadcast(P)).then_inc(s.ctx_in, 16)
            slots = Slots()
            source = {"in": A["w_in"], "ff": A["w_ff"], "out": A["w_out"], "wq": A["w_qof"][0:1],
                      "wo": A["w_qof"][1:2], "wf": A["w_qof"][2:3]}

            last_uses = []

            def use_end(kind, i, c, b):
                return {"in": (s.pm_full, c * FILLS + (4 * i + 8 if i < 2 else 4 * i + 18)),
                        "out": (s.pm_full, c * FILLS + 34), "ff": (s.w3_done, c * FB + i + 1),
                        "wq": (s.q_full, c * KC + KC), "wo": (s.wo_full, 8 * b + 8),
                        "wf": (s.mix_full, 2 * b + 2)}[kind]

            def start_part(it):
                slots.start_part(it)
                last_uses.clear()
                if it is not None:
                    last_uses.extend(use_end(kind, i, 2 * it - 1, it - 1) for kind, i in LOADS_CLOSE[-WSLOTS:])

            def load(kind, i, b, half):
                slot, fills = slots.next()
                if len(last_uses) == WSLOTS:
                    sp.wait_ge(*last_uses.pop(0))
                last_uses.append(use_end(kind, i, 2 * b + half, b))
                n = source[kind].shape[2]
                sp.dma_start(wring[:, slot, 0:n], source[kind][i]).then_inc(w_in[slot], 16)

            def loads(todo, b, half):
                for kind, i in todo:
                    load(kind, i, b, half)

            def front(b, half):
                c = 2 * b + half
                need(sp, s.hn_ready, c)
                sp.dma_start(xm[:, :, :], A["x"][b, half]).then_inc(s.x_in, 16)
                loads(LOADS_FRONT, b, half)
                sp.wait_ge(s.pm_free, c * FILLS + 14)
                sp.dma_start(bc_dram[half], proj[DTR:64, :]).then_inc(s.proj_stored, 16)

            def kv_load(b):
                need(sp, s.wo_full, b * 8)
                sp.wait_ge(s.kv_stored, 32 * BATCH)
                sp.wait_ge(s.zeroed, 2)
                for q in range(4):
                    sp.dma_start(kbd[32 * q:32 * q + 32, :, q * KEYS:(q + 1) * KEYS],
                                 k_dram[b, :, 32 * q:32 * q + 32, :].rearrange("c p k -> p c k")
                                 ).then_inc(s.kv_loaded, 16)
                vv = v_dram[b].rearrange("k (a e d) -> k a e d", e=2, d=DK)
                for e in range(2):
                    sp.dma_start(vbd[64 * e:64 * e + 64, :, DK * e:DK * e + DK], vv[:, :, e, :]
                                 ).then_inc(s.kv_loaded, 16)

            def scan(b, half, k):
                c = 2 * b + half
                if k == STEPS or k % JB:
                    return
                g = k // JB
                if g == 0:
                    sp.wait_ge(s.proj_stored, 16 * (c + 1))
                need(sp, s.p_ready, c * STEPS + (g - 1) * JB)
                need(sp, s.dbu_ready, c * STEPS + (g - 1) * JB)
                for m in range(2):
                    rows = bc_dram[half, m * NS + NP * g:m * NS + NP * g + NP, :]
                    sp.dma_start(bc[:, g % 2, m, :, :], rows.partition_broadcast(P)).then_inc(bc_in[g % 2], 16)
                if half == 1 and g == 0:
                    kv_load(b)

            def close(b, half):
                loads(LOADS_CLOSE, b, half)

            def dense(b, half, kind, i):
                if kind == "mlp":
                    load("ff", i, b, half)
                elif kind == "mlp_last":
                    load("wq", 0, b, half)
                    if half == 1:
                        load("wo", 0, b, half)
                elif kind == "attend" and i == 7:
                    load("wf", 0, b, half)
                elif kind == "norm" and i >= 4:
                    hh = i - 4
                    sp.wait_ge(s.res_done, 2 * b + hh + 1)
                    sp.dma_start(out[b, hh], res[:, hh, :, :]).then_inc(out_stored[hh], 16)

            sp.wait_ge(s.kv_out, KC)
            for c4 in range(KC):
                sp.dma_start(k_dram[:, c4].rearrange("b p k -> p b k"),
                             dtu[:, 4 + c4 // 2, (c4 % 2) * 256:(c4 % 2) * 256 + 256]
                             .rearrange("p (b k) -> p b k", b=BATCH)).then_inc(s.kv_stored, 16)
            sp.wait_ge(s.kv_out, KC + BATCH)
            for b in range(BATCH):
                sp.dma_start(v_dram[b], y[0:KEYS, 1 + b, :]).then_inc(s.kv_stored, 16)
            sp.wait_ge(s.kv_stored, 16 * 2 * BATCH)
            run(sp, (front, scan, close, dense), start_part)
            for hh in range(2):
                sp.wait_ge(out_stored[hh], 16 * BATCH)

        @block.gpsimd
        def _(pool):
            nc.gpsimd.memset(kbd[:, :, :], 0.0).then_inc(s.zeroed, 1)
            nc.gpsimd.memset(vbd[:, :, :], 0.0).then_inc(s.zeroed, 1)
            nc.gpsimd.memset(eps_t[:, :], EPS).then_inc(s.zeroed, 1)
            nc.gpsimd.memset(ones_t[:, :], 1.0).then_inc(s.zeroed, 1)
            nc.gpsimd.memset(zero3[:, :], 0.0).then_inc(s.zeroed, 1)
            nc.gpsimd.memset(t_w2[:, HID:P], 0.0).then_inc(s.zeroed, 1)

            def nothing(*_):
                pass

            def scan(b, half, k):
                if k == STEPS:
                    return
                n = (2 * b + half) * STEPS + k
                if k % JB == 0:
                    need(pool, bc_in[(k // JB) % 2], 32 * ((2 * b + half) * (NG // 2) + k // JB // 2 + 1))
                need(pool, s.h_ready, n + 1)
                nc.gpsimd.tensor_tensor(hb[:, k % 3], hb[:, k % 3], bc[:, (k // JB) % 2, 1], ALU.mult
                                        ).then_inc(s.p_ready, 1)
            run(pool, (nothing, scan, nothing, nothing))

        @block.scalar
        def _(act):
            A_ = nc.scalar.activation
            act.wait_ge(s.const_in, 16 * CONSTS)
            act.wait_ge(s.zeroed, 6)
            A_(a_neg[:, :, :], a_neg[:, :, :], ACT.Exp).then_inc(s.act_front, 1)
            act.wait_ge(s.act_front, 1)
            A_(a_neg[:, :, :], a_neg[:, :, :], ACT.Copy, scale=-1.0).then_inc(s.a_ready, 1)
            for c4 in range(KC):
                act.wait_ge(s.kv_full, c4 + 1)
                A_(dtu[:, 4 + c4 // 2, (c4 % 2) * 256:(c4 % 2) * 256 + 256], pd[:, c4, 0:256], ACT.Identity,
                   bias=bk_c[:, c4:c4 + 1]).then_inc(s.kv_out, 1)
            act.wait_ge(s.a_ready, 2)

            def front(b, half):
                c = 2 * b + half
                f0 = c * FILLS
                act.wait_ge(s.x_in, 16 * (c + 1))
                for t in range(TT):
                    ins = A_(sq_junk[:, t], xm[:, t], ACT.Square, accum_out=small[:, 0, t:t + 1])
                ins.then_inc(s.ss_ready, 1)
                act.wait_ge(s.ss_ready, c + 1)
                A_(small[:, 1, :], small[:, 0, :], ACT.Sqrt, bias=eps_t[:, 0:1], scale=1.0 / DM
                   ).then_inc(s.sd_ready, 1)
                for c4 in range(KC):
                    act.wait_ge(s.pm_full, f0 + c4 + 1)
                    A_(xnT[:, c4], pm[:, c4 % 2], ACT.Copy, scale=norm1[:, c4:c4 + 1]).then_inc(s.pm_free, 1)

                def evacuate(j):
                    r = j % 2
                    act.wait_ge(s.pm_full, f0 + 5 + j)
                    need(act, s.u_ready, c * JB + j - 1)
                    A_(up[:, r, 0:3], halo[:, j] if half else zero3[:, :], ACT.Copy)
                    A_(up[:, r, 3:515], pm[:, j % 2], ACT.Copy)
                    if half == 0:
                        A_(halo[:, j], pm[:, j % 2, CH - 3:CH], ACT.Copy)
                    A_(acc[:, r], pm[:, j % 2], ACT.Identity, bias=conv_b[:, j:j + 1],
                       scale=conv_w[:, j, 3:4]).then_inc(s.pm_free, 1)

                def gate_u(j):
                    act.wait_ge(s.conv_done, c * JB + j + 1)
                    A_(th[:, j % 2], acc[:, j % 2], ACT.Tanh).then_inc(s.th_ready, 1)
                for j in range(JB):
                    evacuate(j)
                    if j:
                        gate_u(j - 1)
                gate_u(JB - 1)
                need(act, s.proj_stored, 16 * c)
                for m in range(2):
                    act.wait_ge(s.pm_full, f0 + 13 + m)
                    A_(proj[:, m * 256:(m + 1) * 256], pm[0:64, m % 2, 0:256], ACT.Copy).then_inc(s.pm_free, 1)
                for j in range(JB):
                    act.wait_ge(s.pm_full, f0 + 15 + j)
                    A_(dt[:, j], pm[:, j % 2], ACT.Identity, bias=dt_b[:, j:j + 1]).then_inc(s.pm_free, 1)
                for q in range(2):
                    act.wait_ge(s.e_min, 2 * c + q + 1)
                    A_(dtu[:, 4 * q:4 * q + 4], dtu[:, 4 * q:4 * q + 4], ACT.Exp).then_inc(s.e_exp, 1)
                    act.wait_ge(s.w1_ready, 2 * c + q + 1)
                    A_(lnp, w1p, ACT.Ln).then_inc(s.ln_ready, 1)

            def scan(b, half, k):
                if k == STEPS:
                    return
                c = 2 * b + half
                n = c * STEPS + k
                g, j = divmod(k, JB)
                if k == 0:
                    act.wait_ge(s.dtu_ready, 2 * (c + 1))
                if k >= 2:
                    need(act, s.h_ready, n - 1)
                for i in range(NP):
                    ins = A_(da[:, k % 2, i], dt[:, j], ACT.Exp, scale=a_neg[:, j, NP * g + i:NP * g + i + 1])
                ins.then_inc(s.da_ready, 1)

            def close(b, half):
                c = 2 * b + half
                f0 = c * FILLS
                act.wait_ge(s.h_ready, (c + 1) * STEPS)
                for j in range(JB):
                    act.wait_ge(s.pm_full, f0 + 23 + j)
                    if j >= 2:
                        need(act, s.gate_done, c * JB + j - 1)
                    A_(zt[:, j % 2], pm[:, j % 2], ACT.Tanh, scale=0.5)
                    A_(zc[:, j % 2], pm[:, j % 2], ACT.Copy, scale=0.5).then_inc(s.pm_free, 1)
                act.wait_ge(s.ht_ready, (c + 1) * TT)
                for t in range(TT):
                    ins = A_(sq_junk[:, t], ht[:, t], ACT.Square, accum_out=small[:, 0, t:t + 1])
                ins.then_inc(s.ss2_ready, 1)
                act.wait_ge(s.ss2_ready, c + 1)
                A_(small[:, 1, :], small[:, 0, :], ACT.Sqrt, bias=eps_t[:, 0:1], scale=1.0 / DM
                   ).then_inc(s.sd2_ready, 1)
                for c4 in range(KC):
                    act.wait_ge(s.pm_full, f0 + 35 + c4)
                    A_(fT[:, c4], pm[:, c4 % 2], ACT.Copy, scale=norm2[:, c4:c4 + 1]).then_inc(s.pm_free, 1)

            def dense(b, half, kind, i):
                c = 2 * b + half
                if kind == "mlp":
                    n = c * FB + i
                    act.wait_ge(s.h1_full, n + 1)
                    need(act, s.hm_ready, n - 1)
                    A_(t1[:, i % 2], ph[:, 0], ACT.Tanh, scale=0.5).then_inc(s.t1_ready, 1)
                elif kind == "norm":
                    n = norm_no(b, i)
                    act.wait_ge(s.ln_var, n + 1)
                    A_(sdev[:, 0, :], mv[:, :, 1], ACT.Sqrt, bias=eps_t[:, 0:1]).then_inc(s.ln_sd, 1)
                elif kind == "turn":
                    for c4 in range(KC):
                        n = (4 * b + i) * KC + c4
                        act.wait_ge(s.tr_full, n + 1)
                        A_(fT[:, c4], pd[:, c4], ACT.Copy).then_inc(s.tr_out, 1)
                elif kind == "query":
                    for c4 in range(KC):
                        act.wait_ge(s.q_full, c * KC + c4 + 1)
                        A_(qT[:, c4, half * CH:(half + 1) * CH], pd[:, c4], ACT.Identity,
                           bias=bq_c[:, c4:c4 + 1]).then_inc(s.q_out, 1)
                elif kind == "stats":
                    n = 16 * b + i
                    act.wait_ge(s.sc_free, n + 1)
                    need(act, s.st_done, 8 * b + i)
                    A_(at, scf[:, i % 2], ACT.Exp, scale=2.0 * DK ** -0.5)
                    A_(scf[:, i % 2], scf[:, i % 2], ACT.Exp, scale=DK ** -0.5).then_inc(s.e_ready, 1)
                elif kind == "temperature":
                    act.wait_ge(s.tm_pe, 4 * b + 1)
                    A_(tmp16[0:3, 0], ph[0:3, 0, 0:HEADS], ACT.Identity, scale=f_sc[:, 0:1],
                       bias=f_sc[:, 1:2]).then_inc(s.tm_act, 1)
                    act.wait_ge(s.tm_pe, 4 * b + 2)
                    A_(tmp16[0:HID, 1], ph[0:HID, 0, 32:32 + HEADS], ACT.Gelu, bias=t_b[0:HID, 0:1]
                       ).then_inc(s.tm_act, 1)
                    act.wait_ge(s.tm_pe, 4 * b + 3)
                    A_(tmp16[0:HID, 2], ph[0:HID, 0, 64:64 + HEADS], ACT.Gelu, bias=t_b[0:HID, 1:2]
                       ).then_inc(s.tm_act, 1)
                    act.wait_ge(s.tm_dve, b + 1)
                    A_(tmp16[:, 3], tmp16[:, 3], ACT.Exp, scale=-1.0).then_inc(s.tm_act, 1)
                elif kind == "score":
                    n = 16 * b + 8 + i
                    act.wait_ge(s.sc_free, n + 1)
                    A_(scf[:, i % 2], scf[:, i % 2], ACT.Exp).then_inc(s.e_ready, 1)
                elif kind == "attend":
                    n = 8 * b + i
                    act.wait_ge(s.pv_full, n + 1)
                    A_(oT[:, :, :].rearrange("p c t -> p (c t)"), pscore[:, i % 2, 0:512], ACT.Copy
                       ).then_inc(s.ot_ready, 1)
                elif kind == "mix":
                    act.wait_ge(s.gl_ready, 2 * b + i + 1)
                    A_(gate[:, 0], gate[:, 0], ACT.Exp).then_inc(s.ge_ready, 1)
                    act.wait_ge(s.gt_full, 2 * b + i + 1)
                    A_(at[:, 0:512], ph[:, 0], ACT.Copy).then_inc(s.gt_ready, 1)
            run(act, (front, scan, close, dense))

        @block.vector
        def _(dve):
            V = nc.vector

            def bcast(ap, n):
                return ap.unsqueeze(len(ap.shape)).broadcast_to([*ap.shape, n])

            dve.wait_ge(s.const_in, 16 * CONSTS)
            V.tensor_scalar(cols[:, 3 * KC:3 * KC + JB], conv_b, 0.5, None, ALU.mult).then_inc(s.a_ready, 1)
            V.tensor_copy(t_w3[:, :], t_w3c[:, :].broadcast_to([HID, P]))
            V.tensor_scalar(conv_w, conv_w, 0.5, None, ALU.mult).then_inc(s.dve_front, 1)
            dve.wait_ge(s.dve_front, 1)
            dve.wait_ge(s.ctx_in, 64)
            for b in range(BATCH):
                dve.wait_ge(s.kv_full, KC + b + 1)
                V.tensor_tensor(y[0:KEYS, 1 + b], pd[0:KEYS, b], y[0:KEYS, 0], ALU.add).then_inc(s.kv_out, 1)
            dve.wait_ge(s.kv_stored, 16 * 2 * BATCH)
            START = 1

            def front(b, half):
                c = 2 * b + half
                f0 = c * FILLS
                ch = Chain(dve, s.dve_front, START + c * DVE_FRONT)
                front.chain = ch
                dve.wait_ge(s.sd_ready, c + 1)
                ch.link(V.reciprocal(small[:, 1, :], small[:, 1, :]))
                for t in range(TT):
                    ins = V.tensor_scalar(y[:, t], xm[:, t], small[:, 1, t:t + 1], None, ALU.mult)
                ins.then_inc(s.xn_ready, 1)

                def gate_u(j):
                    dve.wait_ge(s.th_ready, c * JB + j + 1)
                    V.scalar_tensor_tensor(y[:, j], th[:, j % 2], 1.0, acc[:, j % 2], ALU.add, ALU.mult
                                           ).then_inc(s.u_ready, 1)
                for j in range(JB):
                    r = j % 2
                    dve.wait_ge(s.pm_free, f0 + 5 + j)
                    for tap in (2, 1, 0):
                        ins = V.scalar_tensor_tensor(acc[:, r], up[:, r, tap:tap + CH], conv_w[:, j, tap:tap + 1],
                                                     acc[:, r], ALU.mult, ALU.add)
                        if tap:
                            ch.link(ins)
                    ins.then_inc(s.conv_done, 1)
                    if j:
                        gate_u(j - 1)
                gate_u(JB - 1)
                for q in range(2):
                    jj = slice(4 * q, 4 * q + 4)
                    dve.wait_ge(s.pm_free, f0 + 14 + 4 * q + 4)
                    V.tensor_scalar(dtu[:, jj], dt[:, jj], 20.0, None, ALU.min).then_inc(s.e_min, 1)
                    dve.wait_ge(s.e_exp, 2 * c + q + 1)
                    V.tensor_scalar(w1p, dtu[:, jj], 1.0, None, ALU.add).then_inc(s.w1_ready, 1)
                    dve.wait_ge(s.ln_ready, 2 * c + q + 1)
                    ch.link(V.tensor_scalar(w1p, w1p, -1.0, GUARD, ALU.add, ALU.max))
                    ch.link(V.reciprocal(w1p, w1p))
                    ch.link(V.scalar_tensor_tensor(lnp, lnp, GUARD, w1p, ALU.max, ALU.mult))
                    ch.link(V.tensor_tensor(lnp, lnp, dtu[:, jj], ALU.mult))
                    ch.link(V.tensor_tensor(dt[:, jj], lnp, dt[:, jj], ALU.max))
                    V.tensor_tensor(dtu[:, jj], dt[:, jj], y[:, jj], ALU.mult).then_inc(s.dtu_ready, 1)
                dve.wait_ge(s.dtu_ready, 2 * (c + 1))
                for j in range(JB):
                    ins = V.tensor_scalar(y[:, j], y[:, j], d_skip[:, j:j + 1], None, ALU.mult)
                ins.then_inc(s.y_init, 1)
                dve.wait_ge(s.y_init, c + 1)

            def scan(b, half, k):
                c = 2 * b + half
                n = c * STEPS + k
                g, j = divmod(k, JB)
                if k < STEPS:
                    if j == 0:
                        dve.wait_ge(bc_in[g % 2], 32 * (c * (NG // 2) + g // 2 + 1))
                    need(dve, s.y_added, n - 2)
                    V.tensor_tensor(hb[:, k % 3], dtu[:, j].unsqueeze(1).broadcast_to([P, NP, CH]),
                                    bc[:, g % 2, 0], ALU.mult).then_inc(s.dbu_ready, 1)

                def add(m, i):
                    jm = m % JB
                    V.tensor_tensor(y[:, jm], y[:, jm], hb[:, m % 3, i], ALU.add).then_inc(
                        s.y_added if i else s.y_half, 1)
                if k >= 2:
                    dve.wait_ge(s.p_ready, n - 1)
                    add(k - 2, 0)
                if k < STEPS:
                    dve.wait_ge(s.da_ready, n + 1)
                    dve.wait_ge(s.dbu_ready, n + 1)
                    for i in range(NP):
                        first = state[:, j, NP * g + i:NP * g + i + 1] if half else 0.0
                        ins = V.tensor_tensor_scan(hb[:, k % 3, i], da[:, k % 2, i], hb[:, k % 3, i], first,
                                                   ALU.mult, ALU.add)
                    ins.then_inc(s.h_ready if half else s.scan_done, 1)
                if k >= 2:
                    dve.wait_ge(s.y_half, n - 1)
                    add(k - 2, 1)
                if k < STEPS and half == 0:
                    dve.wait_ge(s.scan_done, b * STEPS + k + 1)
                    V.tensor_copy(state[:, j, NP * g:NP * g + NP], hb[:, k % 3, :, CH - 1]).then_inc(s.h_ready, 1)
                if k == STEPS:
                    dve.wait_ge(s.p_ready, n)
                    add(k - 1, 0)
                    dve.wait_ge(s.y_half, n)
                    add(k - 1, 1)
                    dve.wait_ge(s.y_added, n)

            def close(b, half):
                c = 2 * b + half
                f0 = c * FILLS
                ch = front.chain
                for j in range(JB):
                    dve.wait_ge(s.pm_free, f0 + 23 + j)
                    ch.link(V.scalar_tensor_tensor(zc[:, j % 2], zt[:, j % 2], 1.0, zc[:, j % 2], ALU.add, ALU.mult))
                    V.tensor_tensor(y[:, j], y[:, j], zc[:, j % 2], ALU.mult).then_inc(s.gate_done, 1)
                need(dve, out_stored[half], 16 * b)
                for t in range(TT):
                    dve.wait_ge(s.pm_full, f0 + 31 + t)
                    V.tensor_tensor(ht[:, t], pm[:, t % 2], xm[:, t], ALU.add).then_inc(s.pm_free, 1)
                    dve.wait_ge(s.pm_free, f0 + 31 + t)
                    V.tensor_tensor(res[:, half, t], ht[:, t], xm[:, t], ALU.add).then_inc(s.ht_ready, 1)
                dve.wait_ge(s.sd2_ready, c + 1)
                ch.link(V.reciprocal(small[:, 1, :], small[:, 1, :]))
                for t in range(TT):
                    ins = V.tensor_scalar(ht[:, t], ht[:, t], small[:, 1, t:t + 1], None, ALU.mult)
                ins.then_inc(s.hn_ready, 1)
                assert ch.n == DVE_FRONT, f"DVE_FRONT = {ch.n}"

            def dense(b, half, kind, i):
                c = 2 * b + half
                if (kind, i) == ("mlp", 0):
                    dense.chain = Chain(dve, s.dve_dense, b * (DVE_DENSE0 + DVE_DENSE1) + half * DVE_DENSE0)
                ch = dense.chain
                if kind == "mlp":
                    n = c * FB + i
                    dve.wait_ge(s.t1_ready, n + 1)
                    V.scalar_tensor_tensor(t1[:, i % 2], t1[:, i % 2], 1.0, ph[:, 0], ALU.add, ALU.mult
                                           ).then_inc(s.h1_free, 1)
                    dve.wait_ge(s.h2_full, n + 1)
                    dve.wait_ge(s.h1_free, n + 1)
                    need(dve, s.w3_done, n - 1)
                    V.scalar_tensor_tensor(hm[:, i % 2], t1[:, i % 2], 0.5, ph[:, 1], ALU.mult, ALU.mult
                                           ).then_inc(s.hm_ready, 1)
                elif kind == "mlp_last":
                    dve.wait_ge(s.w3_done, (c + 1) * FB)
                    for t in range(TT):
                        ins = V.tensor_tensor(res[:, half, t], res[:, half, t], pd[:, t], ALU.add)
                    ch.link(ins)
                elif kind == "norm":
                    hh = i % 2
                    for t in range(TT):
                        ins = V.bn_stats(bnst[:, t], res[:, hh, t])
                    ch.link(ins)
                    V.memset(sdev[:, 0, :], 0.0)
                    for t in range(TT):
                        ins = V.bn_aggr(mv[:, t], bnst[:, t])
                    ins.then_inc(s.ln_var, 1)
                    n = norm_no(b, i)
                    dve.wait_ge(s.ln_sd, n + 1)
                    ch.link(V.reciprocal(sdev[:, 1, :], sdev[:, 0, :]))
                    for t in range(TT):
                        ins = V.tensor_scalar(res[:, hh, t], res[:, hh, t], mv[:, t, 0:1], sdev[:, 1, t:t + 1],
                                              ALU.subtract, ALU.mult)
                    if i >= 4:
                        ins.then_inc(s.res_done, 1)
                    else:
                        ins.then_inc(s.ln_done, 1)
                        dve.wait_ge(s.ln_done, 4 * b + i + 1)
                elif kind == "stats":
                    n = 16 * b + i
                    r = i % 2
                    dve.wait_ge(s.sc_full, n + 1)
                    raw = pscore[:, r].rearrange("p (h k) -> p h k", h=HEADS)
                    V.tensor_reduce(stv[:, i, 0], raw, AX, ALU.add)
                    ch.link(V.tensor_reduce(stv[:, i, 1], raw, AX, ALU.max))
                    V.tensor_tensor(sc[:, r], raw, bcast(stv[:, i, 1], KEYS), ALU.subtract).then_inc(s.sc_free, 1)
                    dve.wait_ge(s.e_ready, n + 1)
                    V.tensor_reduce(sden[:, 0], sc[:, r], AX, ALU.add)
                    ch.link(V.tensor_reduce(sden[:, 1], at.rearrange("p (h k) -> p h k", h=HEADS), AX, ALU.add))
                    ch.link(V.reciprocal(sden[:, 0], sden[:, 0]))
                    ch.link(V.tensor_tensor(sden[:, 1], sden[:, 1], sden[:, 0], ALU.mult))
                    V.tensor_tensor(stv[:, i, 2], sden[:, 1], sden[:, 0], ALU.mult).then_inc(s.st_done, 1)
                    dve.wait_ge(s.st_done, 8 * b + i + 1)
                elif kind == "temperature":
                    V.tensor_reduce(sta[:, :, :], stv[:, :, :, :].rearrange("p t k h -> p k h t"), AX, ALU.add
                                    ).then_inc(s.sta_ready, 1)
                    dve.wait_ge(s.tm_pe, 4 * b + 4)
                    ch.link(V.tensor_scalar(tmp16[:, 3], ph[:, 0, 96:96 + HEADS], t_b[:, 2:3], LOG_T, ALU.add, ALU.min))
                    V.tensor_scalar(tmp16[:, 3], tmp16[:, 3], -LOG_T, None, ALU.max).then_inc(s.tm_dve, 1)
                    dve.wait_ge(s.tm_act, 4 * b + 4)
                    for q in range(4):
                        rows = slice(32 * q, 32 * q + 32)
                        ins = V.tensor_scalar(sden[rows, 0, 0:KC], tmp16[rows, 3].rearrange("p (c q) -> p c q", q=4)[:, :, q],
                                              0.5, None, ALU.mult)
                    ch.link(ins)
                    V.tensor_tensor(kbd[:, :, :], kbd[:, :, :], bcast(sden[:, 0, 0:KC], 4 * KEYS), ALU.mult
                                    ).then_inc(s.kb_scaled, 1)
                elif kind == "score":
                    n = 16 * b + 8 + i
                    r = i % 2
                    dve.wait_ge(s.sc_full, n + 1)
                    if i >= 2:
                        dve.wait_ge(s.pt_full, 8 * b + i - 1)
                    dve.wait_ge(s.sc_free, n)
                    raw = pscore[:, r].rearrange("p (h k) -> p h k", h=HEADS)
                    ch.link(V.tensor_reduce(sden[:, 1], raw, AX, ALU.max))
                    V.tensor_tensor(sc[:, r], raw, bcast(sden[:, 1], KEYS), ALU.subtract).then_inc(s.sc_free, 1)
                elif kind == "attend":
                    n = 8 * b + i
                    r = i % 2
                    dve.wait_ge(s.e_ready, 16 * b + 8 + i + 1)
                    ch.link(V.tensor_reduce(sden[:, 0], sc[:, r], AX, ALU.add))
                    ch.link(V.reciprocal(sden[:, 0], sden[:, 0]))
                    V.tensor_tensor(sc[:, r], sc[:, r], bcast(sden[:, 0], KEYS), ALU.mult).then_inc(s.at_norm, 1)
                    dve.wait_ge(s.pt_full, n + 1)
                    if i:
                        dve.wait_ge(s.pv_full, n)
                    V.tensor_scalar(at, phf, 0.0, None, ALU.max).then_inc(s.at_ready, 1)
                    dve.wait_ge(s.wo_full, n + 1)
                    hh, t = divmod(i, TT)
                    V.tensor_tensor(res[:, hh, t], pscore[:, r, 512:1024], res[:, hh, t], ALU.add).then_inc(s.wo_free, 1)
                    dve.wait_ge(s.wo_free, n + 1)
                    ch.link(V.tensor_tensor(res[:, hh, t], res[:, hh, t], bo_row[:, :], ALU.add))
                elif kind == "mix":
                    n = 2 * b + i
                    dve.wait_ge(s.mix_full, n + 1)
                    G = [gate[:, m] for m in range(6)]
                    logits = ph[:, 1, 0:TT * EXPERTS].rearrange("p (t e) -> p t e", e=EXPERTS)
                    rank = rank_w.unsqueeze(1).broadcast_to([P, TT, EXPERTS])

                    def each(ap):
                        return bcast(ap, EXPERTS)
                    ch.link(V.tensor_reduce(gmax[:, :], logits, AX, ALU.max))
                    V.tensor_tensor(G[0], logits, each(gmax[:, :]), ALU.subtract).then_inc(s.gl_ready, 1)
                    dve.wait_ge(s.ge_ready, n + 1)
                    ch.link(V.tensor_reduce(gmax[:, :], G[0], AX, ALU.add))
                    ch.link(V.reciprocal(gmax[:, :], gmax[:, :]))
                    ch.link(V.tensor_tensor(G[1], G[0], each(gmax[:, :]), ALU.mult))
                    ch.link(V.tensor_copy(G[2], G[1]))
                    for m in range(2):
                        ch.link(V.tensor_reduce(gmax[:, :], G[2], AX, ALU.max))
                        ch.link(V.tensor_tensor(G[3], G[2], each(gmax[:, :]), ALU.is_equal))
                        ch.link(V.tensor_tensor(G[3], G[3], rank, ALU.mult))
                        ch.link(V.tensor_reduce(gmax[:, :], G[3], AX, ALU.max))
                        ch.link(V.tensor_tensor(G[4 + m], G[3], each(gmax[:, :]), ALU.is_equal))
                        if m == 0:
                            ch.link(V.scalar_tensor_tensor(G[2], G[4], -2.0, G[2], ALU.mult, ALU.add))
                    ch.link(V.tensor_tensor(G[4], G[4], G[5], ALU.add))
                    ch.link(V.tensor_tensor(G[1], G[1], G[4], ALU.mult))
                    ch.link(V.tensor_reduce(gmax[:, :], G[1], AX, ALU.add))
                    ch.link(V.tensor_scalar(gmax[:, :], gmax[:, :], 1e-6, None, ALU.add))
                    ch.link(V.reciprocal(gmax[:, :], gmax[:, :]))
                    ch.link(V.tensor_tensor(G[1], G[1], each(gmax[:, :]), ALU.mult))
                    V.tensor_tensor(gh[:, :, :, :], ph[:, 0].rearrange("p (t e r) -> p t e r", t=TT, e=EXPERTS),
                                    bcast(G[1], RANK), ALU.mult).then_inc(s.gh_ready, 1)
                    dve.wait_ge(s.mix_done, n + 1)
                    for t in range(TT):
                        ins = V.tensor_tensor(res[:, i, t], pd[:, t], res[:, i, t], ALU.add)
                    ch.link(ins)
                    for t in range(TT):
                        ins = V.tensor_tensor(res[:, i, t], res[:, i, t], ffn_row[:, :], ALU.add)
                    ch.link(ins)
                if (kind, i) in (("stats", 3), ("norm", 5)):
                    want = DVE_DENSE1 if half else DVE_DENSE0
                    assert ch.n == want, f"DVE_DENSE{half} = {ch.n}"
            run(dve, (front, scan, close, dense))

        @block.tensor
        def _(pe):
            M = nc.tensor.matmul
            slots = Slots()

            def use():
                slot, fills = slots.next()
                pe.wait_ge(w_in[slot], 16 * fills)
                return wring[:, slot]

            def group(dst, pairs, start=True, stop=True):
                for n, (a, b) in enumerate(pairs):
                    ins = M(dst, a, b, start=start and n == 0, stop=stop and n == len(pairs) - 1)
                return ins

            pe.wait_ge(s.ctx_in, 64)
            pe.wait_ge(s.const_in, 16 * CONSTS)
            pe.wait_ge(s.zeroed, 6)
            ctxT = dtu[:, 0:2, :].rearrange("p a l -> p (a l)").rearrange("p (c k) -> p c k", c=KC)
            for c4 in range(KC):
                group(pd[:, c4, 0:256], [(dt[:, ci, c4 * P:(c4 + 1) * P], ctxT[:, ci]) for ci in range(KC)]
                      ).then_inc(s.kv_full, 1)
            pe.wait_ge(s.kv_out, KC)
            for b in range(BATCH):
                group(pd[0:KEYS, b], [(ctxT[:, ci, b * KEYS:(b + 1) * KEYS], dt[:, 4 + ci]) for ci in range(KC)]
                      ).then_inc(s.kv_full, 1)
            pe.wait_ge(s.kv_out, KC + BATCH)

            def fill_wait(c, n):
                need(pe, s.pm_free, c * FILLS + n - 1)

            def turn(src, n, c):
                for c4 in range(KC):
                    fill_wait(c, n + c4)
                    for t in range(TT):
                        ins = nc.tensor.transpose(pm[:, c4 % 2, t * P:(t + 1) * P], src[:, t, c4 * P:(c4 + 1) * P],
                                                  ident[:, :])
                    ins.then_inc(s.pm_full, 1)

            def front(b, half):
                c = 2 * b + half
                pe.wait_ge(s.xn_ready, c + 1)
                turn(y, 0, c)
                pe.wait_ge(s.pm_free, c * FILLS + KC)
                for j in range(JB):
                    if j % 4 == 0:
                        w = use().rearrange("p (j c m) -> p j c m", j=4, c=KC)
                    fill_wait(c, 4 + j)
                    ins = group(pm[:, j % 2], [(w[:, j % 4, ci], xnT[:, ci]) for ci in range(KC)])
                    ins.then_inc(s.pm_full, 1)
                pe.wait_ge(s.u_ready, (c + 1) * JB)
                for m in range(2):
                    fill_wait(c, 12 + m)
                    group(pm[0:64, m % 2, 0:256], [(w_x[:, j], y[:, j, m * 256:(m + 1) * 256]) for j in range(JB)]
                          ).then_inc(s.pm_full, 1)
                pe.wait_ge(s.pm_free, c * FILLS + 14)
                for j in range(JB):
                    fill_wait(c, 14 + j)
                    M(pm[:, j % 2], w_dt[:, j * P:(j + 1) * P], proj[0:DTR, :], start=True, stop=True
                      ).then_inc(s.pm_full, 1)

            def scan(b, half, k):
                pass

            def close(b, half):
                c = 2 * b + half
                for j in range(JB):
                    if j % 4 == 0:
                        w = use().rearrange("p (j c m) -> p j c m", j=4, c=KC)
                    fill_wait(c, 22 + j)
                    ins = group(pm[:, j % 2], [(w[:, j % 4, ci], xnT[:, ci]) for ci in range(KC)])
                    ins.then_inc(s.pm_full, 1)
                pe.wait_ge(s.gate_done, (c + 1) * JB)
                w0 = use().rearrange("p (j d) -> p j d", j=4)
                w1 = use().rearrange("p (j d) -> p j d", j=4)
                for t in range(TT):
                    fill_wait(c, 30 + t)
                    ins = group(pm[:, t % 2], [(y[:, j, t * P:(t + 1) * P], (w1 if j >= 4 else w0)[:, j % 4])
                                               for j in range(JB)])
                    ins.then_inc(s.pm_full, 1)
                pe.wait_ge(s.hn_ready, c + 1)
                turn(ht, 34, c)

            def dense(b, half, kind, i):
                c = 2 * b + half
                if kind in ("mlp", "mlp_last"):
                    n = c * FB + i
                    if kind == "mlp":
                        if i == 0:
                            pe.wait_ge(s.pm_free, (c + 1) * FILLS)
                            if half == 0:
                                need(pe, s.res_done, 2 * b)
                            else:
                                pe.wait_ge(s.st_done, 8 * b + 4)
                        w = use()
                        need(pe, s.h1_free, n)
                        group(ph[:, 0], [(w[:, ci * P:(ci + 1) * P], fT[:, ci]) for ci in range(KC)]
                              ).then_inc(s.h1_full, 1)
                        need(pe, s.hm_ready, n)
                        group(ph[:, 1], [(w[:, 512 + ci * P:512 + (ci + 1) * P], fT[:, ci]) for ci in range(KC)]
                              ).then_inc(s.h2_full, 1)
                    if kind == "mlp_last" or i > 0:
                        f = FB - 1 if kind == "mlp_last" else i - 1
                        pe.wait_ge(s.hm_ready, c * FB + f + 1)
                        for t in range(TT):
                            ins = M(pd[:, t], hm[:, f % 2, t * P:(t + 1) * P], dense.w[:, 1024:1536],
                                    start=f == 0, stop=f == FB - 1)
                        ins.then_inc(s.w3_done, 1)
                    if kind == "mlp":
                        dense.w = w
                elif kind == "turn":
                    half_of = i % 2
                    pe.wait_ge(s.ln_done, 4 * b + i + 1)
                    if i == 3:
                        pe.wait_ge(s.ln_var, norm_no(b, 4) + 1)
                    for c4 in range(KC):
                        for t in range(TT):
                            ins = nc.tensor.transpose(pd[:, c4, t * P:(t + 1) * P],
                                                      res[:, half_of, t, c4 * P:(c4 + 1) * P], ident[:, :])
                        ins.then_inc(s.tr_full, 1)
                    pe.wait_ge(s.tr_out, (4 * b + i + 1) * KC)
                elif kind == "query":
                    w = use().rearrange("p (c m) -> p c m", c=KC)
                    for c4 in range(KC):
                        ins = group(pd[:, c4], [(w[:, ci, c4 * P:(c4 + 1) * P], fT[:, ci]) for ci in range(KC)])
                        ins.then_inc(s.q_full, 1)
                    pe.wait_ge(s.q_out, (c + 1) * KC)
                    if half == 0:
                        pe.wait_ge(s.kv_loaded, 96 * (b + 1))
                elif kind in ("stats", "score"):
                    n = 16 * b + i + (8 if kind == "score" else 0)
                    if kind == "stats":
                        if i % 4 >= 2:
                            pe.wait_ge(s.sc_free, n - 1)
                    elif i < 2:
                        pe.wait_ge(s.kb_scaled, b + 1)
                        pe.wait_ge(s.sc_free, 16 * b + 8)
                    else:
                        pe.wait_ge(s.wo_free, 8 * b + i - 1)
                    for c4 in range(KC):
                        ins = M(pscore[:, i % 2, c4 * 256:(c4 + 1) * 256], qT[:, c4, i * P:(i + 1) * P], kbd[:, c4],
                                start=True, stop=True)
                    ins.then_inc(s.sc_full, 1)
                elif kind == "temperature":
                    pe.wait_ge(s.sta_ready, b + 1)
                    for h in range(HEADS):
                        ins = M(ph[0:3, 0, h:h + 1], sta[:, :, h], ones_t[:, :], start=True, stop=True)
                    ins.then_inc(s.tm_pe, 1)
                    pe.wait_ge(s.tm_act, 4 * b + 1)
                    M(ph[0:HID, 0, 32:32 + HEADS], t_w1[:, :], tmp16[0:3, 0], start=True, stop=True).then_inc(s.tm_pe, 1)
                    pe.wait_ge(s.tm_act, 4 * b + 2)
                    M(ph[:, 0, 64:64 + HEADS], t_w2[:, :], tmp16[0:HID, 1], start=True, stop=True).then_inc(s.tm_pe, 1)
                    pe.wait_ge(s.tm_act, 4 * b + 3)
                    M(ph[:, 0, 96:96 + HEADS], t_w3[:, :], tmp16[0:HID, 2], start=True, stop=True).then_inc(s.tm_pe, 1)
                elif kind == "attend":
                    n = 8 * b + i
                    r = i % 2
                    if i == 0:
                        dense.w = use().rearrange("p (c d) -> p c d", c=KC)
                        pe.wait_ge(s.tm_dve, b + 1)
                    pe.wait_ge(s.at_norm, n + 1)
                    if i:
                        pe.wait_ge(s.at_ready, n)
                    for m in range(8):
                        ins = nc.tensor.transpose(phf[:, m * P:(m + 1) * P], scf[:, r, m * P:(m + 1) * P], ident[:, :])
                    ins.then_inc(s.pt_full, 1)
                    pe.wait_ge(s.at_ready, n + 1)
                    for m in range(8):
                        ins = M(pscore[64 * (m % 2):64 * (m % 2) + 64, r, (m // 2) * P:(m // 2 + 1) * P],
                                vbd[:, m], at[:, m * P:(m + 1) * P], start=True, stop=True)
                    ins.then_inc(s.pv_full, 1)
                    pe.wait_ge(s.ot_ready, n + 1)
                    ins = group(pscore[:, r, 512:1024], [(oT[:, c4], dense.w[:, c4]) for c4 in range(KC)])
                    ins.then_inc(s.wo_full, 1)
                elif kind == "mix":
                    n = 2 * b + i
                    if i == 0:
                        dense.w = use().rearrange("p (c d) -> p c d", c=KC)
                    w = dense.w
                    for t in range(TT):
                        group(pd[:, t], [(fT[:, ci, t * P:(t + 1) * P], w[:, ci]) for ci in range(KC)], stop=False)
                    for t in range(TT):
                        group(ph[:, 1, t * EXPERTS:(t + 1) * EXPERTS],
                              [(fT[:, ci, t * P:(t + 1) * P], w_ra[:, ci, 0:EXPERTS]) for ci in range(KC)])
                    for t in range(TT):
                        ins = group(ph[:, 0, t * P:(t + 1) * P],
                                    [(fT[:, ci, t * P:(t + 1) * P], w_ra[:, ci, EXPERTS:EXPERTS + P]) for ci in range(KC)])
                    ins.then_inc(s.mix_full, 1)
                    pe.wait_ge(s.gh_ready, n + 1)
                    for t in range(TT):
                        ins = nc.tensor.transpose(ph[:, 0, t * P:(t + 1) * P], ghf[:, t], ident[:, :])
                    ins.then_inc(s.gt_full, 1)
                    pe.wait_ge(s.gt_ready, n + 1)
                    for t in range(TT):
                        ins = M(pd[:, t], at[:, t * P:(t + 1) * P], w_b[:, :], start=False, stop=True)
                    ins.then_inc(s.mix_done, 1)
            run(pe, (front, scan, close, dense), slots.start_part)


def build(nc, arrays, out_shape):
    A = {n: nc.dram_tensor(f"in_{n}", a.shape, mybir.dt.float32, kind="ExternalInput").ap()
         for n, a in arrays.items()}
    A["x"] = A["x"].rearrange("b (h t p) d -> b h p t d", h=2, p=P)
    out = nc.dram_tensor("out_0", out_shape, mybir.dt.float32, kind="ExternalOutput").ap()
    decoder_layer(nc, A, out.rearrange("b (h t p) d -> b h p t d", h=2, p=P))


def lay_out(i):
    a = {k: np.asarray(v) for k, v in i.items()}
    m, x, f = "L0_attn_", "L0_xattn_", "L0_ffn_"

    def lhs(w):
        return w.T.reshape(-1, P, w.shape[0]).transpose(1, 0, 2)

    def blocks(w):
        return w.reshape(w.shape[0] // P, P, w.shape[1] // P, P).transpose(0, 3, 2, 1)

    def column(v):
        return v.reshape(-1, P).T

    w_in = blocks(a[m + "in_proj_w"]).reshape(4, 4, P, KC, P).transpose(0, 2, 1, 3, 4).reshape(4, P, 2048)
    w_ff = np.concatenate([blocks(a[m + "w1"]).reshape(FB, P, 512), blocks(a[m + "w2"]).reshape(FB, P, 512),
                           a[m + "w3"].T.reshape(FB, P, DM)], axis=2)
    w_out = a[m + "out_proj_w"].T.reshape(2, 4, P, DM).transpose(0, 2, 1, 3).reshape(2, P, 2048)
    rank = np.tile(np.arange(EXPERTS, 0, -1, dtype=np.float32), (P, 1))
    cols = np.concatenate([column(a[m + "norm1_w"]), column(a[m + "norm2_w"]), column(a[x + "bq"]),
                           column(a[m + "conv_b"]), column(a[m + "dt_proj_b"]), column(a[m + "D"]),
                           a[m + "conv_w"].reshape(JB, P, 4).transpose(1, 0, 2).reshape(P, 4 * JB), rank], axis=1)
    ra = np.concatenate([a[f + "R"], a[f + "A"].reshape(P, DM)], axis=0)
    f_sc = np.array([[DK ** -0.5 / (SEQ * KEYS), 0.0], [DK ** -0.5 / SEQ, 0.0],
                     [1.0 / SEQ / (KEYS - 1), -1.0 / KEYS / (KEYS - 1)]], np.float32)
    got = {
        "x": a["x"], "identity": np.eye(P, dtype=np.float32), "w_x": lhs(a[m + "x_proj_w"]),
        "w_dt": a[m + "dt_proj_w"].T, "w_ra": lhs(ra),
        "w_b": a[f + "B"].transpose(0, 2, 1).reshape(P, DM), "bo": a[x + "bo"], "ffn_b": a[f + "b"],
        "cols": cols, "a_log": a[m + "A_log"].reshape(JB, P, NS).transpose(1, 0, 2), "bk_c": column(a[x + "bk"]),
        "t_w1": a[x + "w1"].T, "t_w2": a[x + "w2"].T, "t_w3": a[x + "w3"].T, "t_b1": a[x + "b1"].reshape(HID, 1),
        "t_b2": a[x + "b2"].reshape(HID, 1), "t_b3": a[x + "b3"], "f_sc": f_sc, "bv": a[x + "bv"],
        "ctxT": a["ctx_1024"].reshape(BATCH * KEYS, KC, P).transpose(2, 1, 0).reshape(P, KC * BATCH * KEYS),
        "wk": lhs(a[x + "Wk"]), "wv": lhs(a[x + "Wv"]), "w_in": w_in, "w_ff": w_ff, "w_out": w_out,
        "w_qof": np.stack([lhs(a[x + "Wq"]), lhs(a[x + "Wo"]), lhs(a[f + "W"])]).reshape(3, P, 2048),
    }
    return {k: np.ascontiguousarray(v) for k, v in got.items()}


def kernel(**inputs):
    import concourse.bacc as bacc
    from concourse.bass_utils import run_bass_kernel_spmd

    arrays = lay_out(inputs)
    nc = bacc.Bacc("TRN2", target_bir_lowering=False, num_devices=1)
    build(nc, arrays, inputs["x"].shape)
    r = run_bass_kernel_spmd(nc, [{f"in_{k}": v for k, v in arrays.items()}], core_ids=[0])
    return r.results[0]["out_0"]
```

```python
import numpy as np
import concourse.bass as bass
from concourse import mybir
from contextlib import ExitStack

P = 128
BATCH, SEQ, DM, DI, NS, DTR, DFF = 4, 1024, 512, 1024, 16, 32, 2048
HEADS, KEYS, HID = 16, 64, 64
DK = DM // HEADS
EXPERTS, RANK = 8, 16
CH = 512
CHUNKS = BATCH * SEQ // CH
TT = CH // P
KC = DM // P
JB = DI // P
FB = DFF // P
NP = 2
NG = NS // NP
STEPS = NG * JB
FILLS = 38
FREES = FILLS - TT
MSLOTS = 4
EPS = 1e-5
LOG_T = float(np.log(10.0))
CONSTS = 15

MIXER = ([("load", 0), ("normed", 0), ("turn_in", 0)] + [("conv", j) for j in range(JB + 2)]
         + [("proj", 0), ("step_size", 0), ("exp", 0), ("exp", 1), ("log", 0), ("plus", 0), ("log", 1), ("plus", 1),
            ("skip", 0)]
         + [("step", k) for k in range(STEPS - JB + 1)]
         + [u for j in range(JB) for u in (("step", STEPS - JB + 1 + j), ("z", j))] + [("z", JB)])
MIXER_END = [("out", t) for t in range(TT + 1)] + [("rms", 0), ("normed2", 0), ("turn_out", 0)]
SWIGLU = [("up", 0)] + [u for f in range(FB) for u in (("gate", f), ("up", f + 1))] + [("residual", 0)]


def norm(i):
    return [("var", i), ("scale", i)]


def stats(ts):
    got = [("raw", ts[0])]
    for t in ts:
        got += ([("raw", t + 1)] if t < ts[-1] else []) + [("shift", t), ("sums", t)]
    return got


def attention():
    got = [("score", 0), ("score", 1), ("soft", 0)]
    for t in range(8):
        got += [("weights", t)] + ([("soft", t + 1)] if t < 7 else [])
        got += [("flip", t), ("flipped", t), ("values", t), ("added", t)] + ([("score", t + 2)] if t < 6 else [])
    return got


def mixture(i):
    return [("turn", 2 + i), ("base", i), ("logits", i), ("top2", i), ("lora", i), ("mixed", i)] + norm(4 + i)


DENSE0 = SWIGLU + norm(0) + [("turn", 0), ("query", 0)] + stats(range(4))
DENSE1 = (SWIGLU + norm(1) + [("turn", 1), ("query", 1)] + stats(range(4, 8))
          + [("mean", 0), ("mlp", 0), ("clip", 0), ("temper", 0)] + attention() + norm(2) + norm(3)
          + mixture(0) + mixture(1))
W_X, W_DT, W_Z, W_O, W_END = 4, 5, 6, 10, 14
COST = {"load": 10, "normed": 4, "turn_in": 4, "conv": 5, "proj": 8, "step_size": 8, "exp": 4, "log": 4, "plus": 8,
        "skip": 5, "step": 3.5, "z": 4, "up": 6.5, "gate": 3.5, "residual": 3, "var": 3, "scale": 3, "turn": 4,
        "query": 13, "raw": 1, "shift": 3.5, "sums": 3.5, "mean": 1, "mlp": 6, "clip": 2, "temper": 3, "score": 0.5,
        "soft": 3.5, "weights": 3.5, "flip": 0.5, "flipped": 1, "values": 4, "added": 1.5, "base": 26, "logits": 2,
        "top2": 5, "lora": 5, "mixed": 3}


FRONT_SHARE = 0.3


def weight(kind):
    return COST[kind] * (1 if kind == "step" else FRONT_SHARE)


def merged(dense):
    m_all, d_all = sum(weight(u[0]) for u in MIXER), sum(COST[u[0]] for u in dense)
    got, left, m_sum, d_sum = [], list(dense), 0, 0
    for u in MIXER:
        got.append((True, *u))
        m_sum += weight(u[0])
        while left and d_sum * m_all <= m_sum * d_all:
            d_sum += COST[left[0][0]]
            got.append((False, *left.pop(0)))
    return got + [(False, *u) for u in left] + [(True, *u) for u in MIXER_END]


DVE_MIXER, DVE_DENSE0, DVE_DENSE1 = 32, 19, 99


def need(eng, sem, value):
    if isinstance(value, int) and value <= 0:
        return
    eng.wait_ge(sem, value)


class Chain:

    def __init__(self, eng, sem, start):
        self.eng, self.sem, self.start, self.n = eng, sem, start, 0

    def mark(self, ins):
        self.n += 1
        ins.then_inc(self.sem, 1)

    def settle(self):
        need(self.eng, self.sem, self.start + self.n)

    def link(self, ins):
        self.mark(ins)
        self.settle()


def decoder_layer(nc, A, out):
    f32 = mybir.dt.float32
    ALU = mybir.AluOpType
    ACT = mybir.ActivationFunctionType
    AX = mybir.AxisListType.X
    ctx = ExitStack()
    with ctx:
        def sb(name, shape):
            return ctx.enter_context(nc.sbuf_tensor(name, shape, f32))

        def sem(name):
            return ctx.enter_context(nc.semaphore(name))

        ident = sb("ident", [P, P])
        w_ra = sb("w_ra", [P, KC, EXPERTS + P])
        w_b = sb("w_b", [P, DM])
        bo_row = sb("bo_row", [P, DM])
        ffn_row = sb("ffn_row", [P, DM])
        cols = sb("cols", [P, 2 * KC + 3 * JB + KC + 4 * JB + 8])
        o = 0
        def col(n):
            nonlocal o
            o += n
            return cols[:, o - n:o]
        norm1, norm2, bq_c = col(KC), col(KC), col(KC)
        conv_b, dt_b, d_skip = col(JB), col(JB), col(JB)
        conv_w = col(4 * JB).rearrange("p (j k) -> p j k", k=4)
        rank_w = col(8)
        a_neg = sb("a_neg", [P, JB, NS])
        bk_c = sb("bk_c", [P, KC])
        t_w1 = sb("t_w1", [3, HID])
        t_w2 = sb("t_w2", [HID, P])
        t_w3 = sb("t_w3", [HID, P])
        t_w3c = sb("t_w3c", [HID, 1])
        t_b = sb("t_b", [P, 3])
        f_sc = sb("f_sc", [3, 2])
        eps_t = sb("eps_t", [P, 1])
        ones_t = sb("ones_t", [P, 1])
        zero3 = sb("zero3", [P, 3])
        wmix = sb("wmix", [P, MSLOTS, 1024])
        wdense = sb("wdense", [P, 4096])
        xm = sb("xm", [P, TT, DM])
        xnT = sb("xnT", [P, KC, CH])
        dt = sb("dt", [P, JB, CH])
        dtu = sb("dtu", [P, JB, CH])
        y = sb("y", [P, JB, CH])
        proj = sb("proj", [64, CH])
        bc = sb("bc", [P, 2, 2, NP, CH])
        state = sb("state", [P, JB, NS])
        halo = sb("halo", [P, JB, 3])
        scr = sb("scr", [P, 5120])
        small = sb("small", [P, 2, TT])
        res = sb("res", [P, 2, TT, DM])
        fT = sb("fT", [P, KC, CH])
        qT = sb("qT", [P, KC, SEQ])
        kbd = sb("kbd", [P, KC, 4 * KEYS])
        vbd = sb("vbd", [P, HEADS // 2, 2 * DK])
        work = sb("work", [P, 3072])
        stv = sb("stv", [P, 8, 3, HEADS])
        sta = sb("sta", [P, 3, HEADS])
        sden = sb("sden", [P, 2, HEADS])
        tmp16 = sb("tmp16", [P, 4, HEADS])
        bnst = sb("bnst", [P, TT, 6])
        mv = sb("mv", [P, TT, 2])
        sdev = sb("sdev", [P, 2, TT])
        gate = sb("gate", [P, 6, TT, EXPERTS])
        gmax = sb("gmax", [P, TT])

        w_12 = wdense[:, 0:2048].rearrange("p (r n) -> p r n", r=2)
        w_3 = wdense[:, 2048:3072].rearrange("p (r n) -> p r n", r=2)
        w_qf = wdense[:, 0:2048].rearrange("p (c m) -> p c m", c=KC)
        w_o = wdense[:, 2048:4096].rearrange("p (c m) -> p c m", c=KC)
        da = scr[:, 0:2048].rearrange("p (r n l) -> p r n l", r=2, n=NP)
        hb = scr[:, 2048:5120].rearrange("p (r n l) -> p r n l", r=3, n=NP)
        sq_junk = scr[:, 0:2048].rearrange("p (t d) -> p t d", t=TT)
        up = scr[:, 0:1548].rearrange("p (r l) -> p r l", r=3)
        acc = scr[:, 1548:3084].rearrange("p (r l) -> p r l", r=3)
        th = scr[:, 3084:4108].rearrange("p (r l) -> p r l", r=2)
        w1p = scr[:, 0:2048].rearrange("p (j l) -> p j l", j=4)
        lnp = scr[:, 2048:4096].rearrange("p (j l) -> p j l", j=4)
        zt, zc = bc[:, 0, 0], bc[:, 0, 1]
        ht = scr[:, 2048:4096].rearrange("p (t d) -> p t d", t=TT)
        t1 = work[:, 0:1024].rearrange("p (r l) -> p r l", r=2)
        hm = work[:, 1024:2048].rearrange("p (r l) -> p r l", r=2)
        sc = work[:, 0:2048].rearrange("p (r h k) -> p r h k", r=2, h=HEADS)
        scf = work[:, 0:2048].rearrange("p (r c) -> p r c", r=2)
        at = work[:, 2048:3072]
        oT = sc[:, :, 0:8].rearrange("p r h k -> p r (h k)").rearrange("p r (c t) -> p r c t", c=KC)
        gh = work[:, 0:512].rearrange("p (t e r) -> p t e r", t=TT, e=EXPERTS)
        ghf = work[:, 0:512].rearrange("p (t c) -> p t c", t=TT)

        pm = ctx.enter_context(nc.psum_tensor("pm", [P, 2, 512], f32))
        pd = ctx.enter_context(nc.psum_tensor("pd", [P, 4, 512], f32))
        ph = ctx.enter_context(nc.psum_tensor("ph", [P, 2, 512], f32))
        pscore = pd[:, :, :].rearrange("p (r a) c -> p r (a c)", r=2)
        phf = ph[:, :, :].rearrange("p a c -> p (a c)")

        bc_dram = nc.dram_tensor("bc_dram", (2, 2 * NS, CH), f32, kind="Internal").ap()
        k_dram = nc.dram_tensor("k_dram", (BATCH, KC, P, KEYS), f32, kind="Internal").ap()
        v_dram = nc.dram_tensor("v_dram", (BATCH, KEYS, DM), f32, kind="Internal").ap()

        names = """const_in ctx_in zeroed kv_full kv_out kv_stored kv_loaded x_in ss_ready sd_ready
        xn_ready pm_full pm_free conv_done th_ready u_ready e_abs e_exp w1_ready ln_ready dt_ready dtu_ready y_init
        proj_stored da_ready dbu_ready scan_done h_ready c_times p_ready y_added gate_done ht_ready res_in bias_added ss2_ready
        sd2_ready hn_ready h1_full h1_free t1_ready h2_full hm_ready w3_done ln_var ln_sd ln_done tr_full
        tr_out q_full q_out sc_full sc_free e_ready st_done sta_ready tm_pe tm_act tm_dve kb_scaled at_norm
        pt_full at_ready pv_full ot_ready wo_full wo_free mix_full gl_ready ge_ready gh_ready gt_full
        gt_ready mix_done res_done wq_in wo_in wf_in a_ready dve_front dve_dense act_front""".split()
        S = {n: sem(n) for n in names}
        w12_in = [sem(f"w12_in{i}") for i in range(2)]
        w3_in = [sem(f"w3_in{i}") for i in range(2)]
        wm_in = [sem(f"wm_in{i}") for i in range(MSLOTS)]
        bc_in = [sem(f"bc_in{i}") for i in range(2)]
        out_stored = [sem(f"out_stored{i}") for i in range(2)]
        s = type("Sems", (), S)

        def norm_no(b, i):
            return b * 6 + i

        def body(mixer, dense, b, dense_b):
            for half in range(2):
                stages = DENSE0 if half else DENSE1
                db = b if half else dense_b
                for in_mixer, kind, i in merged([] if db is None else stages):
                    if in_mixer:
                        mixer(b, half, kind, i)
                    else:
                        dense(db, 1 - half, kind, i)

        def run(eng, mixer, dense):
            body(mixer, dense, 0, None)
            with eng.Fori(1, BATCH) as b:
                body(mixer, dense, b, b - 1)
            for kind, i in DENSE1:
                dense(BATCH - 1, 1, kind, i)

        block = ctx.enter_context(nc.Block())

        @block.sync
        def _(sp):
            for dst, src in ((ident[:, :], A["identity"]),
                             (w_ra[:, :, :], A["w_ra"]), (w_b[:, :], A["w_b"]),
                             (bo_row[:, :], A["bo"].partition_broadcast(P)),
                             (ffn_row[:, :], A["ffn_b"].partition_broadcast(P)),
                             (cols[:, :], A["cols"]), (a_neg[:, :, :], A["a_log"]), (bk_c[:, :], A["bk_c"]),
                             (t_w1[:, :], A["t_w1"]), (t_w2[:, 0:HID], A["t_w2"]), (t_w3c[:, :], A["t_w3"]),
                             (t_b[0:HID, 0:1], A["t_b1"]), (t_b[0:HID, 1:2], A["t_b2"]),
                             (t_b[:, 2:3], A["t_b3"].partition_broadcast(P)), (f_sc[:, :], A["f_sc"])):
                sp.dma_start(dst, src).then_inc(s.const_in, 16)
            sp.dma_start(dtu[:, 0:2, :].rearrange("p a l -> p (a l)"), A["ctxT"]).then_inc(s.ctx_in, 16)
            sp.dma_start(dt[:, 0:4, :], A["wk"]).then_inc(s.ctx_in, 16)
            sp.dma_start(dt[:, 4:8, :], A["wv"]).then_inc(s.ctx_in, 16)
            sp.dma_start(y[:, 0, :], A["bv"].partition_broadcast(P)).then_inc(s.ctx_in, 16)

            def load_ff(b, half, f):
                c = 2 * b + half
                if f < 2:
                    if half:
                        sp.wait_ge(s.q_full, c * KC)
                    else:
                        need(sp, s.mix_full, 2 * b)
                else:
                    sp.wait_ge(s.h2_full, c * FB + f - 1)
                sp.dma_start(w_12[:, f % 2], A["w_12"][f]).then_inc(w12_in[f % 2], 16)
                if f < 2 and half == 0:
                    need(sp, s.wo_full, 8 * b)
                elif f < 2:
                    sp.wait_ge(s.w3_done, c * FB)
                else:
                    sp.wait_ge(s.w3_done, c * FB + f - 1)
                sp.dma_start(w_3[:, f % 2], A["w_3"][f]).then_inc(w3_in[f % 2], 16)

            def load_mix(c, n):
                ended = [-4] * 4 + [6, 8, 10, 12, 14, 22, 24, 26, 28, 30]
                need(sp, s.pm_full, c * FILLS + ended[n])
                dst = wmix[:, n % MSLOTS, :]
                if n == W_X:
                    dst, src = dst[:, 0:64 * JB], A["w_x"]
                elif n == W_DT:
                    dst, src = dst[0:DTR], A["w_dt"]
                else:
                    src = A["w_mix"][n if n < W_X else n - 2]
                sp.dma_start(dst, src).then_inc(wm_in[n % MSLOTS], 16)

            def kv_load(b):
                need(sp, s.wo_full, b * 8)
                sp.wait_ge(s.zeroed, 2)
                for q in range(4):
                    sp.dma_start(kbd[32 * q:32 * q + 32, :, q * KEYS:(q + 1) * KEYS],
                                 k_dram[b, :, 32 * q:32 * q + 32, :].rearrange("c p k -> p c k")
                                 ).then_inc(s.kv_loaded, 16)
                vv = v_dram[b].rearrange("k (a e d) -> k a e d", e=2, d=DK)
                for e in range(2):
                    sp.dma_start(vbd[64 * e:64 * e + 64, :, DK * e:DK * e + DK], vv[:, :, e, :]
                                 ).then_inc(s.kv_loaded, 16)

            def mixer(b, half, kind, i):
                c = 2 * b + half
                if kind == "load":
                    need(sp, s.res_in, c * TT)
                    sp.dma_start(xm[:, :, :], A["x"][b, half]).then_inc(s.x_in, 16)
                    for n in range(W_X):
                        load_mix(c, n)
                elif kind == "conv" and i in (4, 6):
                    load_mix(c, W_X if i == 4 else W_DT)
                elif kind == "proj":
                    sp.wait_ge(s.pm_free, c * FREES + 14)
                    sp.dma_start(bc_dram[half], proj[DTR:64, :]).then_inc(s.proj_stored, 16)
                    for n in range(W_Z, W_Z + 3):
                        load_mix(c, n)
                elif kind == "exp" and i == 0:
                    load_mix(c, W_Z + 3)
                elif kind == "step" and i < STEPS and i % JB == 0 or kind == "plus" and i == 1:
                    g = i // JB + 1 if kind == "step" else 0
                    if g == NG:
                        return
                    if g == 0:
                        sp.wait_ge(s.proj_stored, 16 * (c + 1))
                    need(sp, s.p_ready, c * STEPS + (g - 1) * JB)
                    need(sp, s.dbu_ready, c * STEPS + (g - 1) * JB)
                    for m in range(2):
                        rows = bc_dram[half, m * NS + NP * g:m * NS + NP * g + NP, :]
                        sp.dma_start(bc[:, g % 2, m, :, :], rows.partition_broadcast(P)).then_inc(bc_in[g % 2], 16)
                elif kind == "z" and i and i % 2 == 0:
                    load_mix(c, W_O - 1 + i // 2)
                elif kind == "out" and i == 0:
                    load_ff(b, half, 0)
                    load_ff(b, half, 1)
                    if half == 0:
                        kv_load(b)

            def dense(b, half, kind, i):
                c = 2 * b + half
                if kind == "up" and 1 <= i < FB - 1:
                    load_ff(b, half, i + 1)
                elif kind == "up" and i == FB:
                    sp.wait_ge(s.h2_full, (c + 1) * FB)
                    sp.dma_start(w_qf, A["w_qof"][0]).then_inc(s.wq_in, 16)
                    if half:
                        sp.wait_ge(s.w3_done, (c + 1) * FB)
                        sp.dma_start(w_o, A["w_qof"][1]).then_inc(s.wo_in, 16)
                elif kind == "query" and half:
                    sp.wait_ge(s.q_full, (c + 1) * KC)
                    sp.dma_start(w_qf, A["w_qof"][2]).then_inc(s.wf_in, 16)
                elif kind == "scale" and i >= 4:
                    hh = i - 4
                    sp.wait_ge(s.res_done, 2 * b + hh + 1)
                    sp.dma_start(out[b, hh], res[:, hh, :, :]).then_inc(out_stored[hh], 16)

            sp.wait_ge(s.kv_out, KC)
            for c4 in range(KC):
                sp.dma_start(k_dram[:, c4].rearrange("b p k -> p b k"),
                             dtu[:, 4 + c4 // 2, (c4 % 2) * 256:(c4 % 2) * 256 + 256]
                             .rearrange("p (b k) -> p b k", b=BATCH)).then_inc(s.kv_stored, 16)
            sp.wait_ge(s.kv_out, KC + BATCH)
            for b in range(BATCH):
                sp.dma_start(v_dram[b], y[0:KEYS, 1 + b, :]).then_inc(s.kv_stored, 16)
            sp.wait_ge(s.kv_stored, 16 * 2 * BATCH)
            run(sp, mixer, dense)
            for hh in range(2):
                sp.wait_ge(out_stored[hh], 16 * BATCH)

        @block.gpsimd
        def _(pool):
            nc.gpsimd.memset(kbd[:, :, :], 0.0).then_inc(s.zeroed, 1)
            nc.gpsimd.memset(vbd[:, :, :], 0.0).then_inc(s.zeroed, 1)
            nc.gpsimd.memset(eps_t[:, :], EPS).then_inc(s.zeroed, 1)
            nc.gpsimd.memset(ones_t[:, :], 1.0).then_inc(s.zeroed, 1)
            nc.gpsimd.memset(zero3[:, :], 0.0).then_inc(s.zeroed, 1)
            nc.gpsimd.memset(t_w2[:, HID:P], 0.0).then_inc(s.zeroed, 1)

            TTn = nc.gpsimd.tensor_tensor

            def mixer(b, half, kind, i):
                c = 2 * b + half
                if kind == "plus":
                    pool.wait_ge(s.dt_ready, 2 * c + i + 1)
                    TTn(dtu[:, 4 * i:4 * i + 4], dt[:, 4 * i:4 * i + 4], y[:, 4 * i:4 * i + 4], ALU.mult
                        ).then_inc(s.dtu_ready, 1)
                elif kind == "step" and i < STEPS:
                    n = c * STEPS + i
                    g = i // JB
                    if i % JB == 0:
                        pool.wait_ge(bc_in[g % 2], 32 * (c * (NG // 2) + g // 2 + 1))
                    pool.wait_ge(s.h_ready, n + 1)
                    TTn(hb[:, i % 3], hb[:, i % 3], bc[:, g % 2, 1], ALU.mult).then_inc(s.c_times, 1)
                    pool.wait_ge(s.c_times, n + 1)
                    TTn(hb[:, i % 3, 0], hb[:, i % 3, 0], hb[:, i % 3, 1], ALU.add).then_inc(s.p_ready, 1)
                elif kind == "out":
                    if i == 0:
                        need(pool, out_stored[half], 16 * b)
                    else:
                        pool.wait_ge(s.ht_ready, c * TT + i)
                        TTn(res[:, half, i - 1], ht[:, i - 1], xm[:, i - 1], ALU.add).then_inc(s.res_in, 1)

            def dense(b, half, kind, i):
                if (kind, i) in (("query", 0), ("query", 1), ("logits", 0), ("logits", 1)):
                    i += 2 * (kind == "logits")
                    pool.wait_ge(s.tr_full, (4 * b + i + 1) * KC)
                    row = (bo_row if i < 2 else ffn_row)[:, :].unsqueeze(1).broadcast_to([P, TT, DM])
                    TTn(res[:, i % 2], res[:, i % 2], row, ALU.add).then_inc(s.bias_added, 1)
            run(pool, mixer, dense)

        @block.scalar
        def _(act):
            A_ = nc.scalar.activation
            act.wait_ge(s.const_in, 16 * CONSTS)
            act.wait_ge(s.zeroed, 6)
            A_(a_neg[:, :, :], a_neg[:, :, :], ACT.Exp).then_inc(s.act_front, 1)
            act.wait_ge(s.act_front, 1)
            A_(a_neg[:, :, :], a_neg[:, :, :], ACT.Copy, scale=-1.0).then_inc(s.a_ready, 1)
            for c4 in range(KC):
                act.wait_ge(s.kv_full, c4 + 1)
                A_(dtu[:, 4 + c4 // 2, (c4 % 2) * 256:(c4 % 2) * 256 + 256], pd[:, c4, 0:256], ACT.Identity,
                   bias=bk_c[:, c4:c4 + 1]).then_inc(s.kv_out, 1)
            act.wait_ge(s.a_ready, 2)

            def mixer(b, half, kind, i):
                c = 2 * b + half
                f0 = c * FILLS
                if kind == "load":
                    act.wait_ge(s.x_in, 16 * (c + 1))
                    for t in range(TT):
                        ins = A_(sq_junk[:, t], xm[:, t], ACT.Square, accum_out=small[:, 0, t:t + 1])
                    ins.then_inc(s.ss_ready, 1)
                    act.wait_ge(s.ss_ready, c + 1)
                    A_(small[:, 1, :], small[:, 0, :], ACT.Sqrt, bias=eps_t[:, 0:1], scale=1.0 / DM
                       ).then_inc(s.sd_ready, 1)
                elif kind == "turn_in":
                    for c4 in range(KC):
                        act.wait_ge(s.pm_full, f0 + c4 + 1)
                        A_(xnT[:, c4], pm[:, c4 % 2], ACT.Copy, scale=norm1[:, c4:c4 + 1]).then_inc(s.pm_free, 1)
                elif kind == "conv":
                    if i >= 2:
                        j = i - 2
                        act.wait_ge(s.conv_done, c * JB + j + 1)
                        need(act, s.u_ready, c * JB + j - 1)
                        A_(th[:, j % 2], acc[:, j % 3], ACT.Tanh).then_inc(s.th_ready, 1)
                    if i < JB:
                        j, r = i, i % 3
                        act.wait_ge(s.pm_full, f0 + 5 + j)
                        need(act, s.u_ready, c * JB + j - 2)
                        A_(up[:, r, 0:3], halo[:, j] if half else zero3[:, :], ACT.Copy)
                        A_(up[:, r, 3:515], pm[:, j % 2], ACT.Copy)
                        if half == 0:
                            A_(halo[:, j], pm[:, j % 2, CH - 3:CH], ACT.Copy)
                        A_(acc[:, r], pm[:, j % 2], ACT.Identity, bias=conv_b[:, j:j + 1],
                           scale=conv_w[:, j, 3:4]).then_inc(s.pm_free, 1)
                elif kind == "proj":
                    need(act, s.proj_stored, 16 * c)
                    for m in range(2):
                        act.wait_ge(s.pm_full, f0 + 13 + m)
                        A_(proj[:, m * 256:(m + 1) * 256], pm[0:64, m % 2, 0:256], ACT.Copy).then_inc(s.pm_free, 1)
                elif kind == "step_size":
                    for j in range(JB):
                        act.wait_ge(s.pm_full, f0 + 15 + j)
                        A_(dt[:, j], pm[:, j % 2], ACT.Identity, bias=dt_b[:, j:j + 1]).then_inc(s.pm_free, 1)
                elif kind == "exp":
                    jj = slice(4 * i, 4 * i + 4)
                    act.wait_ge(s.pm_free, c * FREES + 22)
                    A_(dtu[:, jj], dt[:, jj], ACT.Abs).then_inc(s.e_abs, 1)
                    act.wait_ge(s.e_abs, 2 * c + i + 1)
                    A_(dtu[:, jj], dtu[:, jj], ACT.Exp, scale=-1.0).then_inc(s.e_exp, 1)
                elif kind == "log":
                    act.wait_ge(s.w1_ready, 2 * c + i + 1)
                    A_(lnp, w1p, ACT.Ln).then_inc(s.ln_ready, 1)
                elif kind == "skip":
                    act.wait_ge(s.dtu_ready, 2 * (c + 1))
                    for j in range(JB):
                        ins = A_(y[:, j], y[:, j], ACT.Copy, scale=d_skip[:, j:j + 1])
                    ins.then_inc(s.y_init, 1)
                elif kind == "step":
                    for k in ((0, 1) if i == 0 else (i + 1,) if i + 1 < STEPS else ()):
                        g, j = divmod(k, JB)
                        if k >= 2:
                            act.wait_ge(s.h_ready, c * STEPS + k - 1)
                        for m in range(NP):
                            ins = A_(da[:, k % 2, m], dt[:, j], ACT.Exp, scale=a_neg[:, j, NP * g + m:NP * g + m + 1])
                        ins.then_inc(s.da_ready, 1)
                elif kind == "z" and i < JB:
                    act.wait_ge(s.pm_full, f0 + 23 + i)
                    if i == 0:
                        act.wait_ge(s.p_ready, (c + 1) * STEPS - JB)
                    if i >= 2:
                        act.wait_ge(s.gate_done, c * JB + i - 1)
                    A_(zt[:, i % 2], pm[:, i % 2], ACT.Tanh, scale=0.5)
                    A_(zc[:, i % 2], pm[:, i % 2], ACT.Copy, scale=0.5).then_inc(s.pm_free, 1)
                elif kind == "out" and i:
                    act.wait_ge(s.ht_ready, c * TT + i)
                    A_(sq_junk[:, i - 1], ht[:, i - 1], ACT.Square, accum_out=small[:, 0, i - 1:i]
                       ).then_inc(s.ss2_ready, 1)
                elif kind == "rms":
                    act.wait_ge(s.ss2_ready, (c + 1) * TT)
                    A_(small[:, 1, :], small[:, 0, :], ACT.Sqrt, bias=eps_t[:, 0:1], scale=1.0 / DM
                       ).then_inc(s.sd2_ready, 1)
                elif kind == "turn_out":
                    for c4 in range(KC):
                        act.wait_ge(s.pm_full, f0 + 35 + c4)
                        A_(fT[:, c4], pm[:, c4 % 2], ACT.Copy, scale=norm2[:, c4:c4 + 1]).then_inc(s.pm_free, 1)

            def dense(b, half, kind, i):
                c = 2 * b + half
                if kind == "gate":
                    n = c * FB + i
                    act.wait_ge(s.h1_full, n + 1)
                    need(act, s.hm_ready, n - 1)
                    A_(t1[:, i % 2], ph[:, 0], ACT.Tanh, scale=0.5).then_inc(s.t1_ready, 1)
                elif kind == "var":
                    act.wait_ge(s.ln_var, norm_no(b, i) + 1)
                    A_(sdev[:, 0, :], mv[:, :, 1], ACT.Sqrt, bias=eps_t[:, 0:1]).then_inc(s.ln_sd, 1)
                elif kind == "turn":
                    for c4 in range(KC):
                        n = (4 * b + i) * KC + c4
                        act.wait_ge(s.tr_full, n + 1)
                        A_(fT[:, c4], pd[:, c4], ACT.Copy).then_inc(s.tr_out, 1)
                elif kind == "query":
                    for c4 in range(KC):
                        act.wait_ge(s.q_full, c * KC + c4 + 1)
                        A_(qT[:, c4, half * CH:(half + 1) * CH], pd[:, c4], ACT.Identity,
                           bias=bq_c[:, c4:c4 + 1]).then_inc(s.q_out, 1)
                elif kind == "shift":
                    act.wait_ge(s.sc_free, 16 * b + i + 1)
                    need(act, s.st_done, 8 * b + i)
                    A_(at, scf[:, i % 2], ACT.Exp, scale=2.0 * DK ** -0.5)
                    A_(scf[:, i % 2], scf[:, i % 2], ACT.Exp, scale=DK ** -0.5).then_inc(s.e_ready, 1)
                elif kind == "mlp":
                    act.wait_ge(s.tm_pe, 4 * b + 1)
                    A_(tmp16[0:3, 0], ph[0:3, 0, 0:HEADS], ACT.Identity, scale=f_sc[:, 0:1],
                       bias=f_sc[:, 1:2]).then_inc(s.tm_act, 1)
                    act.wait_ge(s.tm_pe, 4 * b + 2)
                    A_(tmp16[0:HID, 1], ph[0:HID, 0, 32:32 + HEADS], ACT.Gelu, bias=t_b[0:HID, 0:1]
                       ).then_inc(s.tm_act, 1)
                    act.wait_ge(s.tm_pe, 4 * b + 3)
                    A_(tmp16[0:HID, 2], ph[0:HID, 0, 64:64 + HEADS], ACT.Gelu, bias=t_b[0:HID, 1:2]
                       ).then_inc(s.tm_act, 1)
                elif kind == "clip":
                    act.wait_ge(s.tm_dve, b + 1)
                    A_(tmp16[:, 3], tmp16[:, 3], ACT.Exp, scale=-1.0).then_inc(s.tm_act, 1)
                elif kind == "soft":
                    act.wait_ge(s.sc_free, 16 * b + 8 + i + 1)
                    A_(scf[:, i % 2], scf[:, i % 2], ACT.Exp).then_inc(s.e_ready, 1)
                elif kind == "values":
                    act.wait_ge(s.pv_full, 8 * b + i + 1)
                    A_(oT[:, i % 2].rearrange("p c t -> p (c t)"), pscore[:, i % 2, 0:512], ACT.Copy
                       ).then_inc(s.ot_ready, 1)
                elif kind == "logits":
                    act.wait_ge(s.gl_ready, 2 * b + i + 1)
                    A_(gate[:, 0], gate[:, 0], ACT.Exp).then_inc(s.ge_ready, 1)
                elif kind == "lora":
                    act.wait_ge(s.gt_full, 2 * b + i + 1)
                    A_(at[:, 0:512], ph[:, 0], ACT.Copy).then_inc(s.gt_ready, 1)
            run(act, mixer, dense)

        @block.vector
        def _(dve):
            V = nc.vector

            def bcast(ap, n):
                return ap.unsqueeze(len(ap.shape)).broadcast_to([*ap.shape, n])

            dve.wait_ge(s.const_in, 16 * CONSTS)
            V.tensor_scalar(cols[:, 3 * KC:3 * KC + JB], conv_b, 0.5, None, ALU.mult).then_inc(s.a_ready, 1)
            V.tensor_copy(t_w3[:, :], t_w3c[:, :].broadcast_to([HID, P]))
            V.tensor_scalar(conv_w, conv_w, 0.5, None, ALU.mult).then_inc(s.dve_front, 1)
            dve.wait_ge(s.dve_front, 1)
            dve.wait_ge(s.ctx_in, 64)
            for b in range(BATCH):
                dve.wait_ge(s.kv_full, KC + b + 1)
                V.tensor_tensor(y[0:KEYS, 1 + b], pd[0:KEYS, b], y[0:KEYS, 0], ALU.add).then_inc(s.kv_out, 1)
            dve.wait_ge(s.kv_stored, 16 * 2 * BATCH)
            START = 1

            def mixer(b, half, kind, i):
                c = 2 * b + half
                f0 = c * FILLS
                if kind == "load":
                    mixer.chain = Chain(dve, s.dve_front, START + c * DVE_MIXER)
                ch = mixer.chain
                if kind == "normed":
                    dve.wait_ge(s.sd_ready, c + 1)
                    ch.link(V.reciprocal(small[:, 1, :], small[:, 1, :]))
                    for t in range(TT):
                        ins = V.tensor_scalar(y[:, t], xm[:, t], small[:, 1, t:t + 1], None, ALU.mult)
                    ins.then_inc(s.xn_ready, 1)
                elif kind == "conv":
                    if 1 <= i <= JB:
                        j, r = i - 1, (i - 1) % 3
                        dve.wait_ge(s.pm_free, c * FREES + 5 + j)
                        for tap in (2, 1, 0):
                            ins = V.scalar_tensor_tensor(acc[:, r], up[:, r, tap:tap + CH],
                                                         conv_w[:, j, tap:tap + 1], acc[:, r], ALU.mult, ALU.add)
                            if tap:
                                ch.link(ins)
                        ins.then_inc(s.conv_done, 1)
                    if i >= 2:
                        j = i - 2
                        dve.wait_ge(s.th_ready, c * JB + j + 1)
                        V.scalar_tensor_tensor(y[:, j], th[:, j % 2], 1.0, acc[:, j % 3], ALU.add, ALU.mult
                                               ).then_inc(s.u_ready, 1)
                elif kind == "log":
                    dve.wait_ge(s.e_exp, 2 * c + i + 1)
                    if i:
                        dve.wait_ge(s.dt_ready, 2 * c + 1)
                    V.tensor_scalar(w1p, dtu[:, 4 * i:4 * i + 4], 1.0, None, ALU.add).then_inc(s.w1_ready, 1)
                elif kind == "plus":
                    jj = slice(4 * i, 4 * i + 4)
                    dve.wait_ge(s.ln_ready, 2 * c + i + 1)
                    ch.link(V.scalar_tensor_tensor(lnp, w1p, 1.0, lnp, ALU.is_gt, ALU.mult))
                    ch.link(V.scalar_tensor_tensor(w1p, w1p, -1.0, dtu[:, jj], ALU.add, ALU.subtract))
                    ch.link(V.tensor_tensor(lnp, lnp, w1p, ALU.subtract))
                    V.scalar_tensor_tensor(dt[:, jj], dt[:, jj], 0.0, lnp, ALU.max, ALU.add).then_inc(s.dt_ready, 1)
                elif kind == "step":
                    scan(b, half, i)
                elif kind == "z" and i:
                    j = i - 1
                    dve.wait_ge(s.pm_free, c * FREES + 23 + j)
                    ch.link(V.scalar_tensor_tensor(zc[:, j % 2], zt[:, j % 2], 1.0, zc[:, j % 2], ALU.add, ALU.mult))
                    V.tensor_tensor(y[:, j], y[:, j], zc[:, j % 2], ALU.mult).then_inc(s.gate_done, 1)
                elif kind == "out" and i:
                    t = i - 1
                    dve.wait_ge(s.pm_full, f0 + 31 + t)
                    V.tensor_tensor(ht[:, t], pm[:, t % 2], xm[:, t], ALU.add).then_inc(s.ht_ready, 1)
                elif kind == "normed2":
                    dve.wait_ge(s.sd2_ready, c + 1)
                    dve.wait_ge(s.res_in, (c + 1) * TT)
                    ch.link(V.reciprocal(small[:, 1, :], small[:, 1, :]))
                    for t in range(TT):
                        ins = V.tensor_scalar(ht[:, t], ht[:, t], small[:, 1, t:t + 1], None, ALU.mult)
                    ins.then_inc(s.hn_ready, 1)
                    assert ch.n == DVE_MIXER, f"DVE_MIXER = {ch.n}"

            def scan(b, half, k):
                c = 2 * b + half
                n = c * STEPS + k
                g, j = divmod(k, JB)
                if k < STEPS:
                    if j == 0:
                        dve.wait_ge(bc_in[g % 2], 32 * (c * (NG // 2) + g // 2 + 1))
                    if k == 0:
                        dve.wait_ge(s.dtu_ready, 2 * (c + 1))
                        dve.wait_ge(s.y_init, c + 1)
                    need(dve, s.y_added, n - 2)
                    V.tensor_tensor(hb[:, k % 3], dtu[:, j].unsqueeze(1).broadcast_to([P, NP, CH]),
                                    bc[:, g % 2, 0], ALU.mult).then_inc(s.dbu_ready, 1)

                def add(m):
                    V.tensor_tensor(y[:, m % JB], y[:, m % JB], hb[:, m % 3, 0], ALU.add).then_inc(s.y_added, 1)
                if k >= 2:
                    dve.wait_ge(s.p_ready, n - 1)
                    add(k - 2)
                if k < STEPS:
                    dve.wait_ge(s.da_ready, n + 1)
                    dve.wait_ge(s.dbu_ready, n + 1)
                    for i in range(NP):
                        first = state[:, j, NP * g + i:NP * g + i + 1] if half else 0.0
                        ins = V.tensor_tensor_scan(hb[:, k % 3, i], da[:, k % 2, i], hb[:, k % 3, i], first,
                                                   ALU.mult, ALU.add)
                    ins.then_inc(s.h_ready if half else s.scan_done, 1)
                    if half == 0:
                        dve.wait_ge(s.scan_done, b * STEPS + k + 1)
                        V.tensor_copy(state[:, j, NP * g:NP * g + NP], hb[:, k % 3, :, CH - 1]
                                      ).then_inc(s.h_ready, 1)
                if k == STEPS:
                    dve.wait_ge(s.p_ready, n)
                    add(k - 1)
                    dve.wait_ge(s.y_added, n)

            def dense(b, half, kind, i):
                c = 2 * b + half
                if (kind, i) == ("up", 0):
                    dense.chain = Chain(dve, s.dve_dense, b * (DVE_DENSE0 + DVE_DENSE1) + half * DVE_DENSE0)
                ch = dense.chain
                if kind == "gate":
                    n = c * FB + i
                    dve.wait_ge(s.t1_ready, n + 1)
                    V.scalar_tensor_tensor(t1[:, i % 2], t1[:, i % 2], 1.0, ph[:, 0], ALU.add, ALU.mult
                                           ).then_inc(s.h1_free, 1)
                    dve.wait_ge(s.h2_full, n + 1)
                    dve.wait_ge(s.h1_free, n + 1)
                    need(dve, s.w3_done, n - 1)
                    V.scalar_tensor_tensor(hm[:, i % 2], t1[:, i % 2], 0.5, ph[:, 1], ALU.mult, ALU.mult
                                           ).then_inc(s.hm_ready, 1)
                elif kind == "residual":
                    dve.wait_ge(s.w3_done, (c + 1) * FB)
                    dve.wait_ge(s.res_in, (c + 1) * TT)
                    for t in range(TT):
                        ins = V.tensor_tensor(res[:, half, t], res[:, half, t], pd[:, t], ALU.add)
                    ch.link(ins)
                elif kind == "var":
                    hh = i % 2
                    for t in range(TT):
                        ins = V.bn_stats(bnst[:, t], res[:, hh, t])
                    ch.link(ins)
                    V.memset(sdev[:, 0, :], 0.0)
                    for t in range(TT):
                        ins = V.bn_aggr(mv[:, t], bnst[:, t])
                    ins.then_inc(s.ln_var, 1)
                elif kind == "scale":
                    hh = i % 2
                    dve.wait_ge(s.ln_sd, norm_no(b, i) + 1)
                    ch.link(V.reciprocal(sdev[:, 1, :], sdev[:, 0, :]))
                    for t in range(TT):
                        ins = V.tensor_scalar(res[:, hh, t], res[:, hh, t], mv[:, t, 0:1], sdev[:, 1, t:t + 1],
                                              ALU.subtract, ALU.mult)
                    if i >= 4:
                        ins.then_inc(s.res_done, 1)
                    else:
                        ins.then_inc(s.ln_done, 1)
                        dve.wait_ge(s.ln_done, 4 * b + i + 1)
                elif kind == "shift":
                    n = 16 * b + i
                    r = i % 2
                    dve.wait_ge(s.sc_full, n + 1)
                    raw = pscore[:, r].rearrange("p (h k) -> p h k", h=HEADS)
                    V.tensor_reduce(stv[:, i, 0], raw, AX, ALU.add)
                    ch.link(V.tensor_reduce(stv[:, i, 1], raw, AX, ALU.max))
                    V.tensor_tensor(sc[:, r], raw, bcast(stv[:, i, 1], KEYS), ALU.subtract).then_inc(s.sc_free, 1)
                elif kind == "sums":
                    n = 16 * b + i
                    r = i % 2
                    dve.wait_ge(s.e_ready, n + 1)
                    V.tensor_reduce(sden[:, 0], sc[:, r], AX, ALU.add)
                    ch.link(V.tensor_reduce(sden[:, 1], at.rearrange("p (h k) -> p h k", h=HEADS), AX, ALU.add))
                    ch.link(V.reciprocal(sden[:, 0], sden[:, 0]))
                    ch.link(V.tensor_tensor(sden[:, 1], sden[:, 1], sden[:, 0], ALU.mult))
                    V.tensor_tensor(stv[:, i, 2], sden[:, 1], sden[:, 0], ALU.mult).then_inc(s.st_done, 1)
                    dve.wait_ge(s.st_done, 8 * b + i + 1)
                elif kind == "mean":
                    V.tensor_reduce(sta[:, :, :], stv[:, :, :, :].rearrange("p t k h -> p k h t"), AX, ALU.add
                                    ).then_inc(s.sta_ready, 1)
                elif kind == "clip":
                    dve.wait_ge(s.tm_pe, 4 * b + 4)
                    ch.link(V.tensor_scalar(tmp16[:, 3], ph[:, 0, 96:96 + HEADS], t_b[:, 2:3], LOG_T, ALU.add, ALU.min))
                    V.tensor_scalar(tmp16[:, 3], tmp16[:, 3], -LOG_T, None, ALU.max).then_inc(s.tm_dve, 1)
                elif kind == "temper":
                    dve.wait_ge(s.tm_act, 4 * b + 4)
                    for q in range(4):
                        rows = slice(32 * q, 32 * q + 32)
                        ins = V.tensor_scalar(sden[rows, 0, 0:KC], tmp16[rows, 3].rearrange("p (c q) -> p c q", q=4)[:, :, q],
                                              0.5, None, ALU.mult)
                    ch.link(ins)
                    V.tensor_tensor(kbd[:, :, :], kbd[:, :, :], bcast(sden[:, 0, 0:KC], 4 * KEYS), ALU.mult
                                    ).then_inc(s.kb_scaled, 1)
                elif kind == "soft":
                    n = 16 * b + 8 + i
                    r = i % 2
                    dve.wait_ge(s.sc_full, n + 1)
                    if i >= 2:
                        dve.wait_ge(s.pt_full, 8 * b + i - 1)
                    dve.wait_ge(s.sc_free, n)
                    raw = pscore[:, r].rearrange("p (h k) -> p h k", h=HEADS)
                    ch.link(V.tensor_reduce(sden[:, 1], raw, AX, ALU.max))
                    V.tensor_tensor(sc[:, r], raw, bcast(sden[:, 1], KEYS), ALU.subtract).then_inc(s.sc_free, 1)
                elif kind == "weights":
                    r = i % 2
                    dve.wait_ge(s.e_ready, 16 * b + 8 + i + 1)
                    ch.link(V.tensor_reduce(sden[:, 0], sc[:, r], AX, ALU.add))
                    ch.link(V.reciprocal(sden[:, 0], sden[:, 0]))
                    V.tensor_tensor(sc[:, r], sc[:, r], bcast(sden[:, 0], KEYS), ALU.mult).then_inc(s.at_norm, 1)
                elif kind == "flipped":
                    n = 8 * b + i
                    dve.wait_ge(s.pt_full, n + 1)
                    if i:
                        dve.wait_ge(s.pv_full, n)
                    V.tensor_scalar(at, phf, 0.0, None, ALU.max).then_inc(s.at_ready, 1)
                elif kind == "added":
                    n = 8 * b + i
                    r = i % 2
                    dve.wait_ge(s.wo_full, n + 1)
                    dve.wait_ge(s.bias_added, 4 * b + 2)
                    hh, t = divmod(i, TT)
                    V.tensor_tensor(res[:, hh, t], pscore[:, r, 512:1024], res[:, hh, t], ALU.add).then_inc(s.wo_free, 1)
                elif kind in ("logits", "top2"):
                    n = 2 * b + i
                    G = [gate[:, m] for m in range(6)]
                    logits = ph[:, 1, 0:TT * EXPERTS].rearrange("p (t e) -> p t e", e=EXPERTS)
                    rank = rank_w.unsqueeze(1).broadcast_to([P, TT, EXPERTS])

                    def each(ap):
                        return bcast(ap, EXPERTS)
                    if kind == "logits":
                        dve.wait_ge(s.mix_full, n + 1)
                        ch.link(V.tensor_reduce(gmax[:, :], logits, AX, ALU.max))
                        V.tensor_tensor(G[0], logits, each(gmax[:, :]), ALU.subtract).then_inc(s.gl_ready, 1)
                        return
                    dve.wait_ge(s.ge_ready, n + 1)
                    ch.link(V.tensor_reduce(gmax[:, :], G[0], AX, ALU.add))
                    ch.link(V.reciprocal(gmax[:, :], gmax[:, :]))
                    ch.link(V.tensor_tensor(G[1], G[0], each(gmax[:, :]), ALU.mult))
                    ch.link(V.tensor_copy(G[2], G[1]))
                    for m in range(2):
                        ch.link(V.tensor_reduce(gmax[:, :], G[2], AX, ALU.max))
                        ch.link(V.tensor_tensor(G[3], G[2], each(gmax[:, :]), ALU.is_equal))
                        ch.link(V.tensor_tensor(G[3], G[3], rank, ALU.mult))
                        ch.link(V.tensor_reduce(gmax[:, :], G[3], AX, ALU.max))
                        ch.link(V.tensor_tensor(G[4 + m], G[3], each(gmax[:, :]), ALU.is_equal))
                        if m == 0:
                            ch.link(V.scalar_tensor_tensor(G[2], G[4], -2.0, G[2], ALU.mult, ALU.add))
                    ch.link(V.tensor_tensor(G[4], G[4], G[5], ALU.add))
                    ch.link(V.tensor_tensor(G[1], G[1], G[4], ALU.mult))
                    ch.link(V.tensor_reduce(gmax[:, :], G[1], AX, ALU.add))
                    ch.link(V.tensor_scalar(gmax[:, :], gmax[:, :], 1e-6, None, ALU.add))
                    ch.link(V.reciprocal(gmax[:, :], gmax[:, :]))
                    ch.link(V.tensor_tensor(G[1], G[1], each(gmax[:, :]), ALU.mult))
                    V.tensor_tensor(gh[:, :, :, :], ph[:, 0].rearrange("p (t e r) -> p t e r", t=TT, e=EXPERTS),
                                    bcast(G[1], RANK), ALU.mult).then_inc(s.gh_ready, 1)
                elif kind == "mixed":
                    dve.wait_ge(s.mix_done, 2 * b + i + 1)
                    dve.wait_ge(s.bias_added, 4 * b + 3 + i)
                    for t in range(TT):
                        ins = V.tensor_tensor(res[:, i, t], pd[:, t], res[:, i, t], ALU.add)
                    ch.link(ins)
                if (kind, i) in (("sums", 3), ("scale", 5)):
                    want = DVE_DENSE1 if half else DVE_DENSE0
                    assert ch.n == want, f"DVE_DENSE{half} = {ch.n}"
            run(dve, mixer, dense)

        @block.tensor
        def _(pe):
            M = nc.tensor.matmul

            def use_mix(c, n):
                per_chunk = len(range(n % MSLOTS, W_END, MSLOTS))
                pe.wait_ge(wm_in[n % MSLOTS], 16 * (per_chunk * c + n // MSLOTS + 1))
                return wmix[:, n % MSLOTS]

            def group(dst, pairs, start=True, stop=True):
                for n, (a, b) in enumerate(pairs):
                    ins = M(dst, a, b, start=start and n == 0, stop=stop and n == len(pairs) - 1)
                return ins

            pe.wait_ge(s.ctx_in, 64)
            pe.wait_ge(s.const_in, 16 * CONSTS)
            pe.wait_ge(s.zeroed, 6)
            ctxT = dtu[:, 0:2, :].rearrange("p a l -> p (a l)").rearrange("p (c k) -> p c k", c=KC)
            for c4 in range(KC):
                group(pd[:, c4, 0:256], [(dt[:, ci, c4 * P:(c4 + 1) * P], ctxT[:, ci]) for ci in range(KC)]
                      ).then_inc(s.kv_full, 1)
            pe.wait_ge(s.kv_out, KC)
            for b in range(BATCH):
                group(pd[0:KEYS, b], [(ctxT[:, ci, b * KEYS:(b + 1) * KEYS], dt[:, 4 + ci]) for ci in range(KC)]
                      ).then_inc(s.kv_full, 1)
            pe.wait_ge(s.kv_out, KC + BATCH)

            def fill_wait(c, n):
                need(pe, s.pm_free, c * FREES + n - 1)

            def turn(src, n, c):
                for c4 in range(KC):
                    if n == 0 or c4 >= 2:
                        fill_wait(c, n + c4 if n == 0 else n + c4 - TT)
                    for t in range(TT):
                        ins = nc.tensor.transpose(pm[:, c4 % 2, t * P:(t + 1) * P], src[:, t, c4 * P:(c4 + 1) * P],
                                                  ident[:, :])
                    ins.then_inc(s.pm_full, 1)

            def mixer(b, half, kind, i):
                c = 2 * b + half
                if kind == "turn_in":
                    pe.wait_ge(s.xn_ready, c + 1)
                    turn(y, 0, c)
                elif kind == "conv" and i < JB or kind == "z" and i < JB:
                    n = 0 if kind == "conv" else W_Z
                    if kind == "conv" and i == 0:
                        pe.wait_ge(s.pm_free, c * FREES + KC)
                    if i % 2 == 0:
                        mixer.w = use_mix(c, n + i // 2).rearrange("p (j c m) -> p j c m", j=2, c=KC)
                    n = (4 if kind == "conv" else 22) + i
                    fill_wait(c, n)
                    group(pm[:, n % 2], [(mixer.w[:, i % 2, ci], xnT[:, ci]) for ci in range(KC)]).then_inc(s.pm_full, 1)
                elif kind == "proj":
                    pe.wait_ge(s.u_ready, (c + 1) * JB)
                    w_x = use_mix(c, W_X)[:, 0:64 * JB].rearrange("p (j m) -> p j m", j=JB)
                    for m in range(2):
                        fill_wait(c, 12 + m)
                        group(pm[0:64, m % 2, 0:256], [(w_x[:, j], y[:, j, m * 256:(m + 1) * 256]) for j in range(JB)]
                              ).then_inc(s.pm_full, 1)
                elif kind == "step_size":
                    pe.wait_ge(s.pm_free, c * FREES + 14)
                    w_dt = use_mix(c, W_DT)[0:DTR]
                    for j in range(JB):
                        fill_wait(c, 14 + j)
                        M(pm[:, j % 2], w_dt[:, j * P:(j + 1) * P], proj[0:DTR, :], start=True, stop=True
                          ).then_inc(s.pm_full, 1)
                elif kind == "out" and i < TT:
                    if i == 0:
                        pe.wait_ge(s.gate_done, (c + 1) * JB)
                        mixer.w = [use_mix(c, W_O + n).rearrange("p (j d) -> p j d", j=2) for n in range(4)]
                    if i < 2:
                        fill_wait(c, 30 + i)
                    else:
                        pe.wait_ge(s.ht_ready, c * TT + i - 1)
                    group(pm[:, i % 2], [(y[:, j, i * P:(i + 1) * P], mixer.w[j // 2][:, j % 2]) for j in range(JB)]
                          ).then_inc(s.pm_full, 1)
                elif kind == "turn_out":
                    pe.wait_ge(s.hn_ready, c + 1)
                    turn(ht, 34, c)

            def dense(b, half, kind, i):
                c = 2 * b + half
                if kind == "up":
                    n = c * FB + i
                    if i < FB:
                        if i == 0:
                            pe.wait_ge(s.pm_free, (c + 1) * FREES)
                            if half == 0:
                                need(pe, s.res_done, 2 * b)
                            else:
                                pe.wait_ge(s.st_done, 8 * b + 4)
                        w = w_12[:, i % 2]
                        pe.wait_ge(w12_in[i % 2], 16 * (c * (FB // 2) + i // 2 + 1))
                        need(pe, s.h1_free, n)
                        group(ph[:, 0], [(w[:, ci * P:(ci + 1) * P], fT[:, ci]) for ci in range(KC)]
                              ).then_inc(s.h1_full, 1)
                        need(pe, s.hm_ready, n)
                        group(ph[:, 1], [(w[:, 512 + ci * P:512 + (ci + 1) * P], fT[:, ci]) for ci in range(KC)]
                              ).then_inc(s.h2_full, 1)
                    if i > 0:
                        f = i - 1
                        pe.wait_ge(s.hm_ready, c * FB + f + 1)
                        pe.wait_ge(w3_in[f % 2], 16 * (c * (FB // 2) + f // 2 + 1))
                        for t in range(TT):
                            ins = M(pd[:, t], hm[:, f % 2, t * P:(t + 1) * P], w_3[:, f % 2],
                                    start=f == 0, stop=f == FB - 1)
                        ins.then_inc(s.w3_done, 1)
                elif kind == "turn":
                    half_of = i % 2
                    pe.wait_ge(s.ln_done, 4 * b + i + 1)
                    if i == 3:
                        pe.wait_ge(s.ln_var, norm_no(b, 4) + 1)
                    for c4 in range(KC):
                        for t in range(TT):
                            ins = nc.tensor.transpose(pd[:, c4, t * P:(t + 1) * P],
                                                      res[:, half_of, t, c4 * P:(c4 + 1) * P], ident[:, :])
                        ins.then_inc(s.tr_full, 1)
                    pe.wait_ge(s.tr_out, (4 * b + i + 1) * KC)
                elif kind == "query":
                    w = w_qf
                    pe.wait_ge(s.wq_in, 16 * (c + 1))
                    for c4 in range(KC):
                        ins = group(pd[:, c4], [(w[:, ci, c4 * P:(c4 + 1) * P], fT[:, ci]) for ci in range(KC)])
                        ins.then_inc(s.q_full, 1)
                    pe.wait_ge(s.q_out, (c + 1) * KC)
                    if half == 0:
                        pe.wait_ge(s.kv_loaded, 96 * (b + 1))
                elif kind in ("raw", "score"):
                    n = 16 * b + i + (8 if kind == "score" else 0)
                    if kind == "raw":
                        if i % 4 >= 2:
                            pe.wait_ge(s.sc_free, n - 1)
                    elif i < 2:
                        pe.wait_ge(s.kb_scaled, b + 1)
                        pe.wait_ge(s.sc_free, 16 * b + 8)
                    else:
                        pe.wait_ge(s.wo_free, 8 * b + i - 1)
                    for c4 in range(KC):
                        ins = M(pscore[:, i % 2, c4 * 256:(c4 + 1) * 256], qT[:, c4, i * P:(i + 1) * P], kbd[:, c4],
                                start=True, stop=True)
                    ins.then_inc(s.sc_full, 1)
                elif kind == "mlp":
                    pe.wait_ge(s.sta_ready, b + 1)
                    for h in range(HEADS):
                        ins = M(ph[0:3, 0, h:h + 1], sta[:, :, h], ones_t[:, :], start=True, stop=True)
                    ins.then_inc(s.tm_pe, 1)
                    pe.wait_ge(s.tm_act, 4 * b + 1)
                    M(ph[0:HID, 0, 32:32 + HEADS], t_w1[:, :], tmp16[0:3, 0], start=True, stop=True).then_inc(s.tm_pe, 1)
                    pe.wait_ge(s.tm_act, 4 * b + 2)
                    M(ph[:, 0, 64:64 + HEADS], t_w2[:, :], tmp16[0:HID, 1], start=True, stop=True).then_inc(s.tm_pe, 1)
                    pe.wait_ge(s.tm_act, 4 * b + 3)
                    M(ph[:, 0, 96:96 + HEADS], t_w3[:, :], tmp16[0:HID, 2], start=True, stop=True).then_inc(s.tm_pe, 1)
                elif kind == "flip":
                    n = 8 * b + i
                    r = i % 2
                    if i == 0:
                        pe.wait_ge(s.wo_in, 16 * (b + 1))
                        pe.wait_ge(s.tm_dve, b + 1)
                    pe.wait_ge(s.at_norm, n + 1)
                    if i:
                        pe.wait_ge(s.at_ready, n)
                    for m in range(8):
                        ins = nc.tensor.transpose(phf[:, m * P:(m + 1) * P], scf[:, r, m * P:(m + 1) * P], ident[:, :])
                    ins.then_inc(s.pt_full, 1)
                elif kind == "values":
                    n = 8 * b + i
                    r = i % 2
                    pe.wait_ge(s.at_ready, n + 1)
                    for m in range(8):
                        ins = M(pscore[64 * (m % 2):64 * (m % 2) + 64, r, (m // 2) * P:(m // 2 + 1) * P],
                                vbd[:, m], at[:, m * P:(m + 1) * P], start=True, stop=True)
                    ins.then_inc(s.pv_full, 1)
                    pe.wait_ge(s.ot_ready, n + 1)
                    ins = group(pscore[:, r, 512:1024], [(oT[:, r, c4], w_o[:, c4]) for c4 in range(KC)])
                    ins.then_inc(s.wo_full, 1)
                elif kind == "base":
                    n = 2 * b + i
                    if i == 0:
                        pe.wait_ge(s.wf_in, 16 * (b + 1))
                    w = w_qf
                    for t in range(TT):
                        group(pd[:, t], [(fT[:, ci, t * P:(t + 1) * P], w[:, ci]) for ci in range(KC)], stop=False)
                    for t in range(TT):
                        group(ph[:, 1, t * EXPERTS:(t + 1) * EXPERTS],
                              [(fT[:, ci, t * P:(t + 1) * P], w_ra[:, ci, 0:EXPERTS]) for ci in range(KC)])
                    for t in range(TT):
                        ins = group(ph[:, 0, t * P:(t + 1) * P],
                                    [(fT[:, ci, t * P:(t + 1) * P], w_ra[:, ci, EXPERTS:EXPERTS + P]) for ci in range(KC)])
                    ins.then_inc(s.mix_full, 1)
                elif kind == "lora":
                    n = 2 * b + i
                    pe.wait_ge(s.gh_ready, n + 1)
                    for t in range(TT):
                        ins = nc.tensor.transpose(ph[:, 0, t * P:(t + 1) * P], ghf[:, t], ident[:, :])
                    ins.then_inc(s.gt_full, 1)
                    pe.wait_ge(s.gt_ready, n + 1)
                    for t in range(TT):
                        ins = M(pd[:, t], at[:, t * P:(t + 1) * P], w_b[:, :], start=False, stop=True)
                    ins.then_inc(s.mix_done, 1)
            run(pe, mixer, dense)


def build(nc, arrays, out_shape):
    A = {n: nc.dram_tensor(f"in_{n}", a.shape, mybir.dt.float32, kind="ExternalInput").ap()
         for n, a in arrays.items()}
    A["x"] = A["x"].rearrange("b (h t p) d -> b h p t d", h=2, p=P)
    out = nc.dram_tensor("out_0", out_shape, mybir.dt.float32, kind="ExternalOutput").ap()
    decoder_layer(nc, A, out.rearrange("b (h t p) d -> b h p t d", h=2, p=P))


def lay_out(i):
    a = {k: np.asarray(v) for k, v in i.items()}
    m, x, f = "L0_attn_", "L0_xattn_", "L0_ffn_"

    def lhs(w):
        return w.T.reshape(-1, P, w.shape[0]).transpose(1, 0, 2)

    def blocks(w):
        return w.reshape(w.shape[0] // P, P, w.shape[1] // P, P).transpose(0, 3, 2, 1)

    def column(v):
        return v.reshape(-1, P).T

    w_in = blocks(a[m + "in_proj_w"]).reshape(8, 2, P, KC, P).transpose(0, 2, 1, 3, 4).reshape(8, P, 1024)
    w_12 = np.concatenate([blocks(a[m + "w1"]).reshape(FB, P, 512), blocks(a[m + "w2"]).reshape(FB, P, 512)], axis=2)
    w_out = a[m + "out_proj_w"].T.reshape(4, 2, P, DM).transpose(0, 2, 1, 3).reshape(4, P, 1024)
    rank = np.tile(np.arange(EXPERTS, 0, -1, dtype=np.float32), (P, 1))
    cols = np.concatenate([column(a[m + "norm1_w"]), column(a[m + "norm2_w"]), column(a[x + "bq"]),
                           column(a[m + "conv_b"]), column(a[m + "dt_proj_b"]), column(a[m + "D"]),
                           a[m + "conv_w"].reshape(JB, P, 4).transpose(1, 0, 2).reshape(P, 4 * JB), rank], axis=1)
    ra = np.concatenate([a[f + "R"], a[f + "A"].reshape(P, DM)], axis=0)
    f_sc = np.array([[DK ** -0.5 / (SEQ * KEYS), 0.0], [DK ** -0.5 / SEQ, 0.0],
                     [1.0 / SEQ / (KEYS - 1), -1.0 / KEYS / (KEYS - 1)]], np.float32)
    got = {
        "x": a["x"], "identity": np.eye(P, dtype=np.float32), "w_x": lhs(a[m + "x_proj_w"]).reshape(P, 64 * JB),
        "w_dt": a[m + "dt_proj_w"].T, "w_ra": lhs(ra),
        "w_b": a[f + "B"].transpose(0, 2, 1).reshape(P, DM), "bo": a[x + "bo"], "ffn_b": a[f + "b"],
        "cols": cols, "a_log": a[m + "A_log"].reshape(JB, P, NS).transpose(1, 0, 2), "bk_c": column(a[x + "bk"]),
        "t_w1": a[x + "w1"].T, "t_w2": a[x + "w2"].T, "t_w3": a[x + "w3"].T, "t_b1": a[x + "b1"].reshape(HID, 1),
        "t_b2": a[x + "b2"].reshape(HID, 1), "t_b3": a[x + "b3"], "f_sc": f_sc, "bv": a[x + "bv"],
        "ctxT": a["ctx_1024"].reshape(BATCH * KEYS, KC, P).transpose(2, 1, 0).reshape(P, KC * BATCH * KEYS),
        "wk": lhs(a[x + "Wk"]), "wv": lhs(a[x + "Wv"]), "w_mix": np.concatenate([w_in, w_out]),
        "w_12": w_12, "w_3": a[m + "w3"].T.reshape(FB, P, DM),
        "w_qof": np.stack([lhs(a[x + "Wq"]), lhs(a[x + "Wo"]), lhs(a[f + "W"])]),
    }
    return {k: np.ascontiguousarray(v) for k, v in got.items()}


def kernel(**inputs):
    import concourse.bacc as bacc
    from concourse.bass_utils import run_bass_kernel_spmd

    arrays = lay_out(inputs)
    nc = bacc.Bacc("TRN2", target_bir_lowering=False, num_devices=1)
    build(nc, arrays, inputs["x"].shape)
    r = run_bass_kernel_spmd(nc, [{f"in_{k}": v for k, v in arrays.items()}], core_ids=[0])
    return r.results[0]["out_0"]
```
